# Optimizing a Trainium2 kernel written in Bass

```python
import numpy as np
import jax
import jax.numpy as jnp

def _softmax(x, axis=-1):
    return jax.nn.softmax(x, axis=axis)

def _gelu(x):
    return jax.nn.gelu(x, approximate=True)

def _silu(x):
    return jax.nn.silu(x)

def _sigmoid(x):
    return jax.nn.sigmoid(x)

def _layernorm(x, axis=-1, eps=1e-05):
    m = jnp.mean(x, axis=axis, keepdims=True)
    v = jnp.var(x, axis=axis, keepdims=True)
    return (x - m) / jnp.sqrt(v + eps)

def _scatter_add(tgt, idx, src, axis=0):
    return tgt.at[idx].add(src)

def _segment_sum(src, seg, n):
    return jax.ops.segment_sum(src, seg, n)
kernel_name = 'mk_decoder_preln_d1_seqx_r8_63ef2a'

def setup_inputs(seed: int=0):
    np.random.seed(seed)
    _w = jnp.asarray

    def _rec_inputs():
        import jax
        import jax.numpy as jnp
        _rk = jax.random.key(seed)
        x = 7.22e-05 + 1 * jax.random.normal(jax.random.fold_in(_rk, 1), (16, 256, 128), jnp.float32)
        _lenS = 256 - jax.random.randint(jax.random.fold_in(_rk, 7), (16,), 0, max(1, 256 // 4) + 1, jnp.int32)
        _lenS2 = 64 - jax.random.randint(jax.random.fold_in(_rk, 8), (16,), 0, max(1, 64 // 4) + 1, jnp.int32)
        _ctx_1024P = jax.random.normal(jax.random.fold_in(_rk, 11), (16, 16, 128), jnp.float32)
        _ctx_1024c = jax.random.dirichlet(jax.random.fold_in(_rk, 511), 0.3 * jnp.ones((16,), jnp.float32), (16, 64))
        _ctx_1024t = jnp.einsum('bsk,bkd->bsd', _ctx_1024c, _ctx_1024P)
        _ctx_1024t = _ctx_1024t * jax.lax.rsqrt(jnp.mean(jnp.square(_ctx_1024t)) + 1e-12) * 0.953939
        ctx_1024 = 4.13588e-05 + 0.999923 * (_ctx_1024t + 0.3 * jax.random.normal(jax.random.fold_in(_rk, 611), (16, 64, 128), jnp.float32))
        _validS = jnp.arange(256)[None, :] < _lenS[:, None]
        _validS2 = jnp.arange(64)[None, :] < _lenS2[:, None]
        _causal = jnp.tril(jnp.ones((256, 256), dtype=bool))
        mask_1x1xSxS2_ik0 = jnp.where(jnp.broadcast_to(_validS2[0:1, None, None, :], (1, 1, 256, 64)), 0, 1).astype(jnp.int32)
        return (x, ctx_1024, mask_1x1xSxS2_ik0)
    x, ctx_1024, mask_1x1xSxS2_ik0 = _rec_inputs()

    def _L0_attn_setup():
        import jax, jax.numpy as jnp
        import numpy as np
        from jax import lax
        D_MODEL = 128
        D_INNER = 256
        D_STATE = 16
        D_CONV = 4
        DT_RANK = 64
        B, L = (2, 256)
        LN_EPS = 1e-05

        def _layernorm(x, g, b):
            mu = jnp.mean(x, axis=-1, keepdims=True)
            var = jnp.mean(jnp.square(x - mu), axis=-1, keepdims=True)
            return (x - mu) * lax.rsqrt(var + LN_EPS) * g + b

        def _selective_scan(x_h, dt, Bm, Cm, A):
            b = x_h.shape[0]
            xs = (jnp.swapaxes(x_h, 0, 1), jnp.swapaxes(dt, 0, 1), jnp.swapaxes(Bm, 0, 1), jnp.swapaxes(Cm, 0, 1))
            h0 = jnp.zeros((b, D_INNER, D_STATE), x_h.dtype)

            def step(ht, inp):
                x_t, dt_t, B_t, C_t = inp
                dA = jnp.exp(dt_t[..., None] * A)
                dB = dt_t[..., None] * B_t[:, None, :]
                ht = dA * ht + dB * x_t[..., None]
                y_t = jnp.sum(ht * C_t[:, None, :], axis=-1)
                return (ht, y_t)
            _, ys = lax.scan(step, h0, xs)
            return jnp.swapaxes(ys, 0, 1)
        key = jax.random.key(seed)
        ks = jax.random.split(key, 10)
        s = 0.02
        x = jax.random.normal(ks[0], (B, L, D_MODEL), dtype=jnp.float32)
        ln_g = jnp.ones((D_MODEL,), jnp.float32)
        ln_b = jnp.zeros((D_MODEL,), jnp.float32)
        W_in = jax.random.normal(ks[1], (2 * D_INNER, D_MODEL)) * s
        W_x = jax.random.normal(ks[2], (DT_RANK + 2 * D_STATE, D_INNER)) * s
        W_dt = jax.random.normal(ks[3], (D_INNER, DT_RANK)) * s
        b_dt = jax.random.normal(ks[4], (D_INNER,)) * s
        W_out = jax.random.normal(ks[5], (D_MODEL, D_INNER)) * s
        conv_w = jax.random.normal(ks[6], (D_INNER, 1, D_CONV)) * s
        conv_b = jnp.zeros((D_INNER,), jnp.float32)
        A_log = jnp.log(jnp.tile(jnp.arange(1, D_STATE + 1, dtype=jnp.float32), (D_INNER, 1)))
        D_param = jnp.ones((D_INNER,), jnp.float32)
        alpha = jnp.full((1,), 0.5, jnp.float32)
        return dict(x=x, ln_g=ln_g, ln_b=ln_b, W_in=W_in, W_x=W_x, W_dt=W_dt, b_dt=b_dt, W_out=W_out, conv_w=conv_w, conv_b=conv_b, A_log=A_log, D_param=D_param, alpha=alpha)
    _L0_attn_all = _L0_attn_setup()
    _L0_attn_in = {k: v for k, v in _L0_attn_all.items() if k in ('ln_g', 'ln_b', 'W_in', 'W_x', 'W_dt', 'b_dt', 'W_out', 'conv_w', 'conv_b', 'A_log', 'D_param', 'alpha')}
    del _L0_attn_all

    def _L0_xattn_setup():
        import jax, jax.numpy as jnp
        import numpy as np
        D_MODEL = 128
        N_HEAD = 16
        BATCH = 4
        SEQ = 256
        key = jax.random.key(seed)
        ks = jax.random.split(key, 12)
        s = 1.0 / np.sqrt(D_MODEL)
        inp = {'q': jax.random.normal(ks[0], (BATCH, SEQ, D_MODEL), jnp.float32), 'k': jax.random.normal(ks[1], (BATCH, SEQ, D_MODEL), jnp.float32), 'v': jax.random.normal(ks[2], (BATCH, SEQ, D_MODEL), jnp.float32), 'mask': jnp.tril(jnp.ones((SEQ, SEQ), jnp.int32))[None, None, :, :], 'w_q': jax.random.normal(ks[3], (D_MODEL, D_MODEL), jnp.float32) * s, 'b_q': jax.random.normal(ks[4], (D_MODEL,), jnp.float32) * s, 'w_k': jax.random.normal(ks[5], (D_MODEL, D_MODEL), jnp.float32) * s, 'b_k': jax.random.normal(ks[6], (D_MODEL,), jnp.float32) * s, 'w_v': jax.random.normal(ks[7], (D_MODEL, D_MODEL), jnp.float32) * s, 'b_v': jax.random.normal(ks[8], (D_MODEL,), jnp.float32) * s, 'w_o': jax.random.normal(ks[9], (D_MODEL, D_MODEL), jnp.float32) * s, 'b_o': jax.random.normal(ks[10], (D_MODEL,), jnp.float32) * s}
        return inp
    _L0_xattn_all = _L0_xattn_setup()
    _L0_xattn_in = {k: v for k, v in _L0_xattn_all.items() if k in ('w_q', 'b_q', 'w_k', 'b_k', 'w_v', 'b_v', 'w_o', 'b_o')}
    del _L0_xattn_all

    def _L0_ffn_setup():
        import jax, jax.numpy as jnp
        import numpy as np
        N_EMBD = 128
        N_EXPERTS = 8
        TOP_K = 2
        B, T = (4, 256)
        key = jax.random.key(seed)
        ks = jax.random.split(key, 8)
        C, E, H = (N_EMBD, N_EXPERTS, 4 * N_EMBD)
        s_in = 1.0 / np.sqrt(C)
        s_hid = 1.0 / np.sqrt(H)
        x = jax.random.normal(ks[0], (B, T, C), dtype=jnp.float32)
        W1 = jax.random.uniform(ks[1], (E, C, H), minval=-s_in, maxval=s_in, dtype=jnp.float32)
        b1 = jax.random.uniform(ks[2], (E, H), minval=-s_in, maxval=s_in, dtype=jnp.float32)
        W2 = jax.random.uniform(ks[3], (E, H, C), minval=-s_hid, maxval=s_hid, dtype=jnp.float32)
        b2 = jax.random.uniform(ks[4], (E, C), minval=-s_hid, maxval=s_hid, dtype=jnp.float32)
        Wg = jax.random.uniform(ks[5], (C, E), minval=-s_in, maxval=s_in, dtype=jnp.float32)
        bg = jax.random.uniform(ks[6], (E,), minval=-s_in, maxval=s_in, dtype=jnp.float32)
        return {'x': x, 'W1': W1, 'b1': b1, 'W2': W2, 'b2': b2, 'Wg': Wg, 'bg': bg}
    _L0_ffn_all = _L0_ffn_setup()
    _L0_ffn_in = {k: v for k, v in _L0_ffn_all.items() if k in ('W1', 'b1', 'W2', 'b2', 'Wg', 'bg')}
    del _L0_ffn_all
    return {'x': x, 'ctx_1024': ctx_1024, 'mask_1x1xSxS2_ik0': mask_1x1xSxS2_ik0, 'L0_attn_ln_g': _L0_attn_in['ln_g'], 'L0_attn_ln_b': _L0_attn_in['ln_b'], 'L0_attn_W_in': _L0_attn_in['W_in'], 'L0_attn_W_x': _L0_attn_in['W_x'], 'L0_attn_W_dt': _L0_attn_in['W_dt'], 'L0_attn_b_dt': _L0_attn_in['b_dt'], 'L0_attn_W_out': _L0_attn_in['W_out'], 'L0_attn_conv_w': _L0_attn_in['conv_w'], 'L0_attn_conv_b': _L0_attn_in['conv_b'], 'L0_attn_A_log': _L0_attn_in['A_log'], 'L0_attn_D_param': _L0_attn_in['D_param'], 'L0_attn_alpha': _L0_attn_in['alpha'], 'L0_xattn_w_q': _L0_xattn_in['w_q'], 'L0_xattn_b_q': _L0_xattn_in['b_q'], 'L0_xattn_w_k': _L0_xattn_in['w_k'], 'L0_xattn_b_k': _L0_xattn_in['b_k'], 'L0_xattn_w_v': _L0_xattn_in['w_v'], 'L0_xattn_b_v': _L0_xattn_in['b_v'], 'L0_xattn_w_o': _L0_xattn_in['w_o'], 'L0_xattn_b_o': _L0_xattn_in['b_o'], 'L0_ffn_W1': _L0_ffn_in['W1'], 'L0_ffn_b1': _L0_ffn_in['b1'], 'L0_ffn_W2': _L0_ffn_in['W2'], 'L0_ffn_b2': _L0_ffn_in['b2'], 'L0_ffn_Wg': _L0_ffn_in['Wg'], 'L0_ffn_bg': _L0_ffn_in['bg']}

def reference(x, ctx_1024, mask_1x1xSxS2_ik0, L0_attn_ln_g, L0_attn_ln_b, L0_attn_W_in, L0_attn_W_x, L0_attn_W_dt, L0_attn_b_dt, L0_attn_W_out, L0_attn_conv_w, L0_attn_conv_b, L0_attn_A_log, L0_attn_D_param, L0_attn_alpha, L0_xattn_w_q, L0_xattn_b_q, L0_xattn_w_k, L0_xattn_b_k, L0_xattn_w_v, L0_xattn_b_v, L0_xattn_w_o, L0_xattn_b_o, L0_ffn_W1, L0_ffn_b1, L0_ffn_W2, L0_ffn_b2, L0_ffn_Wg, L0_ffn_bg):
    import jax
    import jax.numpy as jnp

    def _L0_attn_ref(x, ln_g, ln_b, W_in, W_x, W_dt, b_dt, W_out, conv_w, conv_b, A_log, D_param, alpha):
        import jax, jax.numpy as jnp
        import numpy as np
        from jax import lax
        D_MODEL = 128
        D_INNER = 256
        D_STATE = 16
        D_CONV = 4
        DT_RANK = 64
        B, L = (2, 256)
        LN_EPS = 1e-05

        def _layernorm(x, g, b):
            mu = jnp.mean(x, axis=-1, keepdims=True)
            var = jnp.mean(jnp.square(x - mu), axis=-1, keepdims=True)
            return (x - mu) * lax.rsqrt(var + LN_EPS) * g + b

        def _selective_scan(x_h, dt, Bm, Cm, A):
            b = x_h.shape[0]
            xs = (jnp.swapaxes(x_h, 0, 1), jnp.swapaxes(dt, 0, 1), jnp.swapaxes(Bm, 0, 1), jnp.swapaxes(Cm, 0, 1))
            h0 = jnp.zeros((b, D_INNER, D_STATE), x_h.dtype)

            def step(ht, inp):
                x_t, dt_t, B_t, C_t = inp
                dA = jnp.exp(dt_t[..., None] * A)
                dB = dt_t[..., None] * B_t[:, None, :]
                ht = dA * ht + dB * x_t[..., None]
                y_t = jnp.sum(ht * C_t[:, None, :], axis=-1)
                return (ht, y_t)
            _, ys = lax.scan(step, h0, xs)
            return jnp.swapaxes(ys, 0, 1)
        residual = x
        h = _layernorm(x, ln_g, ln_b)
        x_and_res = h @ W_in.T
        x_h, res = jnp.split(x_and_res, [D_INNER], axis=-1)
        xc = jnp.swapaxes(x_h, 1, 2)
        xc = lax.conv_general_dilated(xc, conv_w, window_strides=(1,), padding=[(D_CONV - 1, 0)], dimension_numbers=('NCH', 'OIH', 'NCH'), feature_group_count=D_INNER)
        xc = xc + conv_b[None, :, None]
        x_h = jax.nn.silu(jnp.swapaxes(xc, 1, 2))
        x_dbl = x_h @ W_x.T
        dt, Bm, Cm = jnp.split(x_dbl, [DT_RANK, DT_RANK + D_STATE], axis=-1)
        dt = jax.nn.softplus(dt @ W_dt.T + b_dt)
        A = -jnp.exp(A_log)
        y = _selective_scan(x_h, dt, Bm, Cm, A) + x_h * D_param
        y = y * jax.nn.silu(res)
        out = y @ W_out.T
        return residual + alpha * out

    def _L0_xattn_ref(q, k, v, mask, w_q, b_q, w_k, b_k, w_v, b_v, w_o, b_o):
        import jax, jax.numpy as jnp
        import numpy as np
        D_MODEL = 128
        N_HEAD = 16
        BATCH = 4
        SEQ = 256
        batch, q_len, d_model = q.shape
        k_len = k.shape[1]
        n_d = d_model // N_HEAD
        qh = (q @ w_q.T + b_q).reshape(batch, q_len, N_HEAD, n_d).transpose(0, 2, 1, 3)
        kh = (k @ w_k.T + b_k).reshape(batch, k_len, N_HEAD, n_d).transpose(0, 2, 1, 3)
        vh = (v @ w_v.T + b_v).reshape(batch, k_len, N_HEAD, n_d).transpose(0, 2, 1, 3)
        score = jnp.einsum('bhqd,bhkd->bhqk', qh, kh) / jnp.sqrt(jnp.float32(n_d))
        score = jnp.where(mask == 0, jnp.float32(-1000000000.0), score)
        attn = jax.nn.softmax(score, axis=-1)
        out = jnp.einsum('bhqk,bhkd->bhqd', attn, vh)
        out = out.transpose(0, 2, 1, 3).reshape(batch, q_len, d_model)
        return out @ w_o.T + b_o

    def _L0_ffn_ref(x, W1, b1, W2, b2, Wg, bg):
        import jax, jax.numpy as jnp
        import numpy as np
        N_EMBD = 128
        N_EXPERTS = 8
        TOP_K = 2
        B, T = (4, 256)
        gate_scores = jax.nn.softmax(jnp.einsum('btc,ce->bte', x, Wg) + bg, axis=-1)
        h = jax.nn.relu(jnp.einsum('btc,ech->bteh', x, W1) + b1)
        expert_out = jnp.einsum('bteh,ehc->btec', h, W2) + b2
        topk_scores, topk_idx = jax.lax.top_k(gate_scores, TOP_K)
        top_probs = jax.nn.softmax(topk_scores, axis=-1)
        sel = jnp.take_along_axis(expert_out, topk_idx[..., None], axis=2)
        out = jnp.sum(sel * top_probs[..., None], axis=2)
        return out
    x = x + _L0_attn_ref(_layernorm(x, axis=-1), L0_attn_ln_g, L0_attn_ln_b, L0_attn_W_in, L0_attn_W_x, L0_attn_W_dt, L0_attn_b_dt, L0_attn_W_out, L0_attn_conv_w, L0_attn_conv_b, L0_attn_A_log, L0_attn_D_param, L0_attn_alpha)
    x = x + _L0_xattn_ref(_layernorm(x, axis=-1), ctx_1024, ctx_1024, mask_1x1xSxS2_ik0, L0_xattn_w_q, L0_xattn_b_q, L0_xattn_w_k, L0_xattn_b_k, L0_xattn_w_v, L0_xattn_b_v, L0_xattn_w_o, L0_xattn_b_o)
    x = x + _L0_ffn_ref(_layernorm(x, axis=-1), L0_ffn_W1, L0_ffn_b1, L0_ffn_W2, L0_ffn_b2, L0_ffn_Wg, L0_ffn_bg)
    return x

_drawn_inputs = setup_inputs


def setup_inputs(seed=0):
    import zlib

    import numpy as np

    out = dict(_drawn_inputs(seed))
    spreads = {'L0_attn_ln_g': (1.0, 0.6),
     'L0_attn_ln_b': (0.0, 0.8),
     'L0_attn_conv_b': (0.0, 0.8),
     'L0_attn_D_param': (1.0, 0.6)}
    factors = {'L0_attn_W_in': 8.0,
     'L0_attn_W_x': 8.0,
     'L0_attn_W_dt': 8.0,
     'L0_attn_b_dt': 8.0,
     'L0_attn_W_out': 8.0,
     'L0_attn_conv_w': 8.0,
     'L0_attn_A_log': 8.0,
     'L0_xattn_b_q': 27.968,
     'L0_xattn_b_k': 200.0,
     'L0_ffn_b1': 200.0,
     'L0_ffn_b2': 200.0,
     'ctx_1024': 8.0,
     'L0_xattn_w_q': 8.0,
     'L0_xattn_w_k': 8.0,
     'L0_xattn_w_v': 8.0,
     'L0_xattn_b_v': 37.964,
     'L0_xattn_w_o': 8.0,
     'L0_xattn_b_o': 64.0,
     'L0_ffn_W1': 25.634,
     'L0_ffn_W2': 8.0,
     'L0_ffn_Wg': 8.0,
     'L0_ffn_bg': 64.0}
    for name, (base, spread) in spreads.items():
        noise = np.random.default_rng([zlib.crc32(name.encode()), seed]).standard_normal(out[name].shape)
        drawn = base * np.exp(spread * noise) if base else spread * noise
        out[name] = jnp.asarray(drawn.astype(out[name].dtype))
    for name, factor in factors.items():
        out[name] = (out[name] * factor).astype(out[name].dtype)
    return out
```

```python
import concourse.bass as bass
from concourse import mybir
from contextlib import ExitStack

ALU = mybir.AluOpType
ACT = mybir.ActivationFunctionType
BF16 = mybir.dt.bfloat16
F32 = mybir.dt.float32
I32 = mybir.dt.int32
U32 = mybir.dt.uint32
AX = mybir.AxisListType

P = 128
BATCH, SEQ, D = 16, 256, 128
DI, NST, DTR, TAPS = 256, 16, 64, 4
KEYS, HEADS, HD = 64, 16, 8
EXPERTS, HID = 8, 512
NB = 2
TOK = NB * SEQ
ROUNDS = BATCH // NB
DT = DI // P
NC = 4
CHUNKS = NB * NST // NC
STEPS = CHUNKS * DT
HP = HEADS // 2
VW = 2 * HD + 2
QT = SEQ // P
HC = HID // P
EPS = 1e-5
MASKED = -1e9


class Marks:

    def __init__(self, sem, names):
        self.sem, self.names = sem, names.split()

    def at(self, name, r):
        return r * len(self.names) + self.names.index(name) + 1

    def all(self, r):
        return (r + 1) * len(self.names)


def decoder(nc, x, ctx_in, mask, ln_g, ln_b, W_in, W_x, W_dt, b_dt, W_out, conv_w, conv_b, A_log, D_param,
            alpha, w_q, b_q, w_k, b_k, w_v, b_v, w_o, b_o, W1, b1, W2, b2, Wg, bg,
            c_ident, c_center, c_mean, c_pick, c_pickmax, c_blk, c_iota, out):
    with ExitStack() as es:
        def sb(name, shape, dt=F32):
            return es.enter_context(nc.sbuf_tensor(name, shape, dt))

        def ps(name, shape, dt=F32):
            return es.enter_context(nc.psum_tensor(name, shape, dt))

        def sem(name):
            return es.enter_context(nc.semaphore(name))

        ident = sb("ident", [P, P])
        identb = sb("identb", [P, P], BF16)
        center = sb("center", [P, P])
        mean = sb("mean", [P, P])
        sel = sb("sel", [96, 2 * NST, P], BF16)
        selmax = sb("selmax", [96, HP, P], BF16)
        pick = sb("pick", [96, 2 * NST])
        pickmax = sb("pickmax", [96, HEADS])
        blk = sb("blk", [P, HEADS])
        iota = sb("iota", [P, EXPERTS])
        E = sb("E", [P, NB, HP, SEQ])
        spare = E[:, :, :, :].rearrange("p b g s -> p (b g s)")
        took = [0]

        def borrow(rows, cols):
            took[0] += cols
            return spare[0:rows, took[0] - cols:took[0]]

        win_nat = borrow(P, 4 * D).rearrange("p (n d) -> p n d", n=4)
        wx_nat = borrow(96, DI)
        wdt_nat = borrow(P, DT * DTR).rearrange("p (n r) -> p n r", n=DT)
        wout_nat = borrow(P, DI)
        att_nat = borrow(P, 4 * D).rearrange("p (n d) -> p n d", n=4)
        b1_nat = borrow(EXPERTS * HC, P)
        winT = sb("winT", [P, DT * TAPS + DT, P])
        wdtrT = sb("wdtrT", [P, DT, DTR])
        wbcT = sb("wbcT", [P, DT, 3, 2 * NST])
        wdtT = sb("wdtT", [DTR, DT, P])
        woutT = sb("woutT", [P, DT, P])
        attT = sb("attT", [P, 4, P])
        b1T = sb("b1T", [P, EXPERTS * HC])
        win_tap = borrow(P, DT * TAPS * D).rearrange("p (i d) -> p i d", d=D)
        gv = sb("gv", [P, 1])
        bv_ = sb("bv_", [P, 1])
        convw = sb("convw", [P, DT, TAPS])
        convb = sb("convb", [P, DT])
        bdt = sb("bdt", [P, DT])
        alog = sb("alog", [P, DT, NST])
        Aneg = sb("Aneg", [P, DT, NST])
        dpar = sb("dpar", [P, DT])
        alph = sb("alph", [P, 1])
        bq = sb("bq", [P, 1])
        bk = sb("bk", [P, 1])
        bo = sb("bo", [P, 1])
        bvrow = sb("bvrow", [1, D])
        onerow = sb("onerow", [1, P])
        epsc = sb("epsc", [P, 1])
        idle = sb("idle", [P, 2])
        onec = sb("onec", [P, 1])
        mask_i = sb("mask_i", [P, QT, KEYS], I32)
        keep = sb("keep", [P, QT, KEYS])
        kany = sb("kany", [P, QT])
        kanyb = borrow(P, QT * P).rearrange("p (t m) -> p t m", t=QT)
        KA = sb("KA", [P, SEQ])
        mbias = sb("mbias", [P, QT, KEYS], BF16)
        mbias2 = sb("mbias2", [P, QT, 2, KEYS], BF16)
        w1s = sb("w1s", [P, EXPERTS, HID])
        w2s = spare.rearrange("p (e j c) -> p e j c", e=EXPERTS, j=HC)
        b2s = sb("b2s", [EXPERTS, D])
        wgs = sb("wgs", [P, EXPERTS])
        bgrow = sb("bgrow", [1, EXPERTS])

        xin = sb("xin", [P, TOK // P, D])
        xT = sb("xT", [P, TOK])
        sq = sb("sq", [P, TOK])
        rstd = sb("rstd", [P, TOK])
        xn = sb("xn", [P, TOK])
        xn2 = sb("xn2", [P, TOK])
        hpad = sb("hpad", [P, NB, TAPS - 1 + SEQ])
        xh = sb("xh", [P, 2, DT, TOK])
        sres = sb("sres", [P, 2, DT, TOK])
        dtr = sb("dtr", [DTR, TOK])
        S = sb("S", [96, 2, TOK], BF16)
        left = sb("left", [96, TOK])
        soft = sb("soft", [P, DT, TOK])
        zpos = sb("zpos", [P, DT, TOK])
        dtm = sb("dtm", [P, 2, DT, TOK])
        dtx = sb("dtx", [P, 2, DT, TOK])
        xres = sb("xres", [P, 2, TOK])

        dA = sb("dA", [P, 2, NC, SEQ])
        Bs = sb("Bs", [P, 2, NC, SEQ])
        u = sb("u", [P, 2, NC, SEQ])
        hst = sb("hst", [P, 2, NC, SEQ])
        prod = sb("prod", [P, 2, NC, SEQ])
        yd = sb("yd", [P, DT, SEQ])
        gy = sb("gy", [P, DT, TOK])
        x1T = sb("x1T", [P, TOK])

        cin = sb("cin", [P, D])
        cT = sb("cT", [P, NB, KEYS])
        cT2 = sb("cT2", [P, NB, 2, KEYS])
        KT = sb("KT", [P, NB, KEYS])
        Kbd = sb("Kbd", [P, NB, HEADS, KEYS])
        Vbd = sb("Vbd", [P, NB, HP, VW])
        qT = sb("qT", [P, NB, SEQ])
        xq = sb("xq", [P, TOK])
        sqt = sb("sqt", [P, TOK])
        rstdt = sb("rstdt", [P, TOK])
        mx = sb("mx", [P, NB * QT, HEADS])
        mleft = sb("mleft", [P, NB * QT, HEADS])
        nm = sb("nm", [P, NB * QT, 3, 32], BF16)
        nmT = sb("nmT", [96, NB * SEQ], BF16)
        rden = sb("rden", [P, NB, QT * HP, 2])
        on2 = sb("on2", [P, NB * QT, HP, 2, HD])
        oT = sb("oT", [P, NB, SEQ])
        x2o = sb("x2o", [P, TOK])
        x2d = nc.dram_tensor("x2d", (ROUNDS, P, TOK), F32).ap()

        x2c = [xin[:, :, :].rearrange("p t d -> p (t d)"), xT[:, :]]
        xf = [xn2, xn]
        lg = sb("lg", [P, TOK // P, EXPERTS])
        pr = sb("pr", [P, TOK // P, EXPERTS])
        lmax = sb("lmax", [P, TOK // P])
        lsum = sb("lsum", [P, TOK // P])
        top = sb("top", [P, TOK // P, 8])
        topi = sb("topi", [P, TOK // P, 8], U32)
        topf = sb("topf", [P, TOK // P, 2])
        gap = sb("gap", [P, TOK // P])
        wt = sb("wt", [P, 2, TOK // P])
        hot = sb("hot", [P, 2, TOK // P, EXPERTS])
        wsel = sb("wsel", [P, 2, TOK // P, EXPERTS])
        wselT = sb("wselT", [EXPERTS, TOK])
        hid = [t[:, :, :, :].rearrange("p a n s -> p (a n s)").rearrange("p (j t) -> p j t", j=HC) for t in (hst, prod)]
        acc = [xres[:, i, :].rearrange("p (t d) -> p t d", d=D) for i in range(2)]

        Cp = ps("Cp", [P, NC, SEQ])
        Bp = ps("Bp", [P, 2, SEQ])
        Y = ps("Y", [P, DT, SEQ])
        M = [ps("M0", [P, 512]), ps("M1", [P, 512])]
        T = [ps("T0", [P, 512]), ps("T1", [P, 512])]

        Hid = [M[0][:, :], M[1][:, :]] + [Cp[:, 2 * i:2 * i + 2, :].rearrange("p n s -> p (n s)") for i in range(2)]
        G = [t[:, :, :].rearrange("p n s -> p (n s)") for t in (Bp, Y)]
        Tb = T[0][:, :].bitcast(BF16)

        s_w = sem("s_w")
        s_tr = sem("s_tr")
        s_tc = sem("s_tc")
        s_pre = sem("s_pre")
        s_prea = sem("s_prea")
        s_pres = sem("s_pres")
        s_w2 = sem("s_w2")
        s_x = sem("s_x")
        s_c = sem("s_c")
        Ap = Marks(sem("Ap"), "tr cen1 var1 cen2 var2 cv0 cv1 rs0 rs1 wx wbc dt0 dt1")
        Aa = Marks(sem("Aa"), "xT sq1 ln1 rs1 sq2 ln2 rs2 h0 xh0 xh1 sr0 sr1 dtr S1 S2 S3 az0 ea0 L0 az1 ea1 L1")
        Av = Marks(sem("Av"), "xn h0a r1 r2 zp0 zp1")
        Ag = Marks(sem("Ag"), "xr dt0 dx0 dt1 dx1")
        s_bp = sem("s_bp")
        s_bs = sem("s_bs")
        s_cp = sem("s_cp")
        s_ex = sem("s_ex")
        s_u = sem("s_u")
        s_sc = sem("s_sc")
        s_pd = sem("s_pd")
        s_ns = sem("s_ns")
        s_yd = sem("s_yd")
        s_gy = sem("s_gy")
        s_wo = sem("s_wo")
        s_x1 = sem("s_x1")
        Tp = Marks(sem("Tp"), "ctr kv cen var q s0 s1 s2 s3 m st00 st01 st10 st11 o t wo")
        Ta = Marks(sem("Ta"), "cT cT2 KT v sq ln rs m e00 e01 e10 e11 t")
        Tv = Marks(sem("Tv"), "xq q mx0 mx1 mx2 mx3 ma mb mc md me r n x2")
        Tg = Marks(sem("Tg"), "kb0 kb1")
        Fp = Marks(sem("Fp"), "cen var g x2 wT b2")
        Fa = Marks(sem("Fa"), "sq ln rs e ge wT")
        s_h = sem("s_h")
        s_hr = sem("s_hr")
        s_o = sem("s_o")
        s_ac = sem("s_ac")
        Fv = Marks(sem("Fv"), "xf mx sb x2 pe0 rs pr " + " ".join(f"{w}{t}" for w in "ti" for t in range(TOK // P))
                   + " tf gap gs w0 w1 h0 h1 g0 g1 wsel b2")
        s_x2 = sem("s_x2")
        s_x2in = [sem(f"s_x2in{q}") for q in range(2)]
        s_out = [sem(f"s_out{q}") for q in range(2)]

        xd = x.rearrange("b s d -> (b s) d")
        od = out.rearrange("b s d -> (b s) d")
        cd = ctx_in.rearrange("b k d -> (b k) d")

        loads = [
            (ident[:, :], c_ident), (center[:, :], c_center), (mean[:, :], c_mean),
            (win_nat[:, :, :], W_in.rearrange("(n p) d -> p n d", p=P)),
            (convw[:, :, :], conv_w.rearrange("(n p) o k -> p n (o k)", p=P)),
            (wx_nat[:, :], W_x), (wdt_nat[:, :, :], W_dt.rearrange("(n p) r -> p n r", p=P)),
            (wout_nat[:, :], W_out),
            (gv[:, :], ln_g.rearrange("(p o) -> p o", o=1)), (bv_[:, :], ln_b.rearrange("(p o) -> p o", o=1)),
            (convb[:, :], conv_b.rearrange("(n p) -> p n", p=P)), (bdt[:, :], b_dt.rearrange("(n p) -> p n", p=P)),
            (alog[:, :, :], A_log.rearrange("(n p) s -> p n s", p=P)),
            (dpar[:, :], D_param.rearrange("(n p) -> p n", p=P)),
            (alph[:, :], alpha.partition_broadcast(P)),
            (pick[:, :], c_pick), (pickmax[:, :], c_pickmax), (blk[:, :], c_blk), (iota[:, :], c_iota),
            (att_nat[:, 0, :], w_q), (att_nat[:, 1, :], w_k), (att_nat[:, 2, :], w_v), (att_nat[:, 3, :], w_o),
            (bq[:, :], b_q.rearrange("(p o) -> p o", o=1)), (bk[:, :], b_k.rearrange("(p o) -> p o", o=1)),
            (bo[:, :], b_o.rearrange("(p o) -> p o", o=1)), (bvrow[:, :], b_v.rearrange("(o d) -> o d", o=1)),
            (mask_i[:, :, :], mask.rearrange("a b (t p) k -> p (a b t) k", p=P)),
            (b1_nat[:, :], b1.rearrange("e (j p) -> (e j) p", p=P)), (b2s[:, :], b2), (wgs[:, :], Wg),
            (bgrow[:, :], bg.rearrange("(o e) -> o e", o=1)),
            (w1s[:, :, :], W1.rearrange("e c h -> c e h")),
        ]
        WALL = 16 * len(loads)

        turns = [(win_tap[:, i, :], winT[:, i, :], P, P) for i in range(DT * TAPS)]
        turns += [(win_nat[:, DT + i, :], winT[:, DT * TAPS + i, :], P, P) for i in range(DT)]
        turns += [(wx_nat[:, i * P:(i + 1) * P], i, 96, P) for i in range(DT)]
        turns += [(wdt_nat[:, i, :], wdtT[:, i, :], P, DTR) for i in range(DT)]
        turns += [(wout_nat[:, i * P:(i + 1) * P], woutT[:, i, :], P, P) for i in range(DT)]
        turns += [(att_nat[:, i, :], attT[:, i, :], P, P) for i in range(4)]
        turns += [(b1_nat[:, :], b1T[:, :], EXPERTS * HC, P)]
        NTURN = len(turns)
        NPRE = 1 + DT * TAPS + 13

        block = es.enter_context(nc.Block())

        def rounds(eng, body, drain):
            body(0, 0, nxt=True, prev=False, tail=False)
            body(1, 1, nxt=True, prev=True, tail=False)
            with eng.Fori(2, ROUNDS - 2, 2) as r:
                body(r, 0, nxt=True, prev=True, tail=True)
                body(r + 1, 1, nxt=True, prev=True, tail=True)
            body(ROUNDS - 2, 0, nxt=True, prev=True, tail=True)
            body(ROUNDS - 1, 1, nxt=False, prev=True, tail=True)
            for k in range(STEPS):
                drain(ROUNDS, 0, k, nxt=False, prev=True, tail=True)
            for k in range(2):
                drain(ROUNDS + 1, 1, k, nxt=False, prev=False, tail=True)

        def expert_rounds(eng, body):
            body(0, 0, nxt=True)
            with eng.Fori(1, ROUNDS - 1, 2) as r:
                body(r, 1, nxt=True)
                body(r + 1, 0, nxt=True)
            body(ROUNDS - 1, 1, nxt=False)

        NTT = TOK // P
        TRIO = ((0, 1), (4, 5)), ((2, 3), (6, 7))

        def step_of(k):
            return k // (STEPS // NB), (k // DT) % (NST // NC), k % DT

        @block.sync
        def _(sp):
            for dst, src in loads:
                sp.dma_start(dst, src, allow_slow_non_contiguous=True).then_inc(s_w, 16)

            def load_x(r):
                if not isinstance(r, int) or r:
                    sp.wait_ge(Ap.sem, Ap.at("tr", r - 1))
                sp.dma_start(xin[:, :, :], xd[bass.ds(r * TOK, TOK), :].rearrange("(n p) d -> p n d", p=P)).then_inc(s_x, 16)

            def load_c(r):
                if not isinstance(r, int) or r:
                    sp.wait_ge(Tp.sem, Tp.at("ctr", r - 1))
                sp.dma_start(cin[:, :], cd[bass.ds(r * NB * KEYS, NB * KEYS), :]).then_inc(s_c, 16)

            def store_x2(r):
                sp.wait_ge(Tv.sem, Tv.all(r))
                sp.dma_start(x2d[r, :, :] if isinstance(r, int) else x2d[bass.ds(r, 1), :, :].rearrange("o p t -> p (o t)"), x2o[:, :]).then_inc(s_x2, 16)

            sp.sem_inc(s_x2, 16)
            load_x(0)
            load_c(0)
            load_x(1)
            load_x(2)
            load_c(1)
            with sp.Fori(3, ROUNDS) as r:
                load_x(r)
                load_c(r - 1)
                store_x2(r - 3)
            load_c(ROUNDS - 1)
            store_x2(ROUNDS - 3)
            store_x2(ROUNDS - 2)
            sp.wait_ge(Tp.sem, Tp.at("o", ROUNDS - 1))
            sp.dma_start(w2s[:, :, :, :], W2.rearrange("e (j p) c -> p e j c", p=P)).then_inc(s_w2, 16)
            store_x2(ROUNDS - 1)
            sp.wait_ge(s_x2, 16 * (ROUNDS + 1))

            def load_x2(r, q):
                if not isinstance(r, int) or r >= 2:
                    sp.wait_ge(Fp.sem, Fp.at("x2", r - 2))
                src = x2d[r, :, :] if isinstance(r, int) else x2d[bass.ds(r, 1), :, :].rearrange("o p t -> p (o t)")
                sp.dma_start(x2c[q], src).then_inc(s_x2in[q], 16)

            def store(r, q):
                sp.wait_ge(s_ac, (r + 1) * EXPERTS * NTT)
                sp.dma_start(od[bass.ds(r * TOK, TOK), :].rearrange("(n p) d -> p n d", p=P), acc[q]).then_inc(s_out[q], 16)

            load_x2(0, 0)
            load_x2(1, 1)
            with sp.Fori(0, ROUNDS // 2 - 1) as h:
                for q in range(2):
                    load_x2(2 * h + 2 + q, q)
                    store(2 * h + q, q)
            store(ROUNDS - 2, 0)
            store(ROUNDS - 1, 1)
            for q in range(2):
                sp.wait_ge(s_out[q], 8 * ROUNDS)

        @block.tensor
        def _(pe):
            def mm(o, l, r_, start=True, stop=True, **kw):
                return pe.matmul(o, l, r_, start=start, stop=stop, **kw)

            pe.wait_ge(s_w, WALL)
            pe.wait_ge(s_pre, 1 + DT * TAPS)
            for i, (src, _, rows, cols) in enumerate(turns):
                if i >= 2:
                    pe.wait_ge(s_tc, i - 1)
                pe.transpose(T[i % 2][0:cols, 0:rows], src, ident[0:rows, 0:rows]).then_inc(s_tr, 1)
            pe.wait_ge(s_tc, NTURN)
            pe.wait_ge(s_pre, NPRE)
            for t in range(QT):
                m = mm(T[0][:, t * P:(t + 1) * P], kanyb[:, t, :], ident[:, :])
            m.then_inc(s_tr, 1)
            pe.wait_ge(s_pre, NPRE + 1)

            def turn_x(r):
                pe.wait_ge(s_x, 16 * (r + 1))
                for t in range(NTT):
                    m = pe.transpose(M[1][:, t * P:(t + 1) * P], xin[:, t, :], ident[:, :])
                m.then_inc(Ap.sem, 1)

            def center_x(r, n):
                if n == 1:
                    pe.wait_ge(Aa.sem, Aa.at("xT", r))
                    mm(M[0][:, :], center[:, :], xT[:, :]).then_inc(Ap.sem, 1)
                else:
                    pe.wait_ge(Av.sem, Av.at("xn", r))
                    mm(M[0][:, :], center[:, :], xn[:, :]).then_inc(Ap.sem, 1)

            def variance_x(r, n):
                pe.wait_ge(Aa.sem, Aa.at(f"sq{n}", r))
                mm(M[1][:, :], mean[:, :], sq[:, :]).then_inc(Ap.sem, 1)

            def conv(r):
                pe.wait_ge(Aa.sem, Aa.at("h0", r))
                for d in range(DT):
                    for k in range(TAPS):
                        m = mm(M[d][:, :], winT[:, d * TAPS + k, :], hpad[:, :, k:k + SEQ], start=k == 0, stop=k == TAPS - 1)
                    m.then_inc(Ap.sem, 1)

            def gate_in(r):
                for d in range(DT):
                    pe.wait_ge(Aa.sem, Aa.at(f"xh{d}", r))
                    mm(M[d][:, :], winT[:, DT * TAPS + d, :], hpad[:, :, TAPS - 1:TAPS - 1 + SEQ]).then_inc(Ap.sem, 1)

            def x_states(r, q):
                pe.wait_ge(Aa.sem, Aa.at("sr0", r))
                for d in range(DT):
                    m = mm(M[0][0:DTR, :], wdtrT[:, d, :], xh[:, q, d, :], start=d == 0, stop=d == DT - 1)
                m.then_inc(Ap.sem, 1)
                pe.wait_ge(Aa.sem, Aa.at("sr1", r))
                for d in range(DT):
                    m = mm(M[1][0:96, :], wbcT[:, d, :, :], xh[:, q, d, :], start=d == 0, stop=d == DT - 1)
                m.then_inc(Ap.sem, 1)

            def steps_in(r):
                pe.wait_ge(Aa.sem, Aa.at("dtr", r))
                mm(M[0][:, :], wdtT[:, 0, :], dtr[:, :]).then_inc(Ap.sem, 1)
                pe.wait_ge(Av.sem, Av.at("r1", r))
                mm(M[1][:, :], wdtT[:, 1, :], dtr[:, :]).then_inc(Ap.sem, 1)

            def spread_b(r, q, j):
                g = r * CHUNKS + j
                b, c = divmod(j, NST // NC)
                if j == 0:
                    pe.wait_ge(Aa.sem, Aa.at("S3", r))
                for half in range(2):
                    if half or j or not isinstance(r, int) or r:
                        pe.wait_ge(s_bs, 2 * g + half)
                    for i in range(2):
                        n = c * NC + 2 * half + i
                        m = mm(Bp[:, i, :], sel[:, n, :], S[:, q, b * SEQ:(b + 1) * SEQ])
                    m.then_inc(s_bp, 1)

            def spread_c(r, q, j):
                g = r * CHUNKS + j
                b, c = divmod(j, NST // NC)
                if j or not isinstance(r, int) or r:
                    pe.wait_ge(s_pd, 2 * g)
                for i in range(NC):
                    m = mm(Cp[:, i, :], sel[:, NST + c * NC + i, :], S[:, q, b * SEQ:(b + 1) * SEQ])
                m.then_inc(s_cp, 1)

            def sum_states(r, q, k):
                b, c, d = step_of(k)
                if c == 0 and d == 0 and (b or not isinstance(r, int) or r):
                    pe.wait_ge(s_yd, r * 4 + 2 * b)
                pe.wait_ge(s_pd, r * STEPS + k + 1)
                for i in range(NC):
                    m = mm(Y[:, d, :], ident[:, :], prod[:, k % 2, i, :], start=c == 0 and d == 0 and i == 0,
                           stop=c == 3 and i == NC - 1, skip_group_check=True)
                m.then_inc(s_ns, 1)

            def mixer_out(r):
                pe.wait_ge(s_gy, 4 * (r + 1))
                for d in range(DT):
                    m = mm(M[0][:, :], woutT[:, d, :], gy[:, d, :], start=d == 0, stop=d == DT - 1)
                m.then_inc(s_wo, 1)

            def turn_c(r):
                pe.wait_ge(s_c, 16 * (r + 1))
                pe.transpose(T[0][:, 0:P], cin[:, :], ident[:, :]).then_inc(Tp.sem, 1)

            def keys_values(r):
                pe.wait_ge(Ta.sem, Ta.at("cT2", r))
                if not isinstance(r, int) or r:
                    pe.wait_ge(Tv.sem, Tv.at("x2", r - 1))
                mm(T[1][:, 0:P], attT[:, 1, :], cT[:, :, :])
                for b in range(NB):
                    o = T[1][:, (b + 1) * P:(b + 2) * P]
                    mm(o, cT2[:, b, :, :], attT[:, 2, :], stop=False)
                    m = mm(o, onerow[:, :], bvrow[:, :], start=False)
                m.then_inc(Tp.sem, 1)

            def att_center(r):
                pe.wait_ge(s_x1, r + 1)
                mm(T[0][:, :], center[:, :], x1T[:, :]).then_inc(Tp.sem, 1)

            def att_variance(r):
                pe.wait_ge(Ta.sem, Ta.at("sq", r))
                mm(T[1][:, :], mean[:, :], sqt[:, :]).then_inc(Tp.sem, 1)

            def queries(r):
                pe.wait_ge(Tv.sem, Tv.at("xq", r))
                mm(T[1][:, :], attT[:, 0, :], xq[:, :]).then_inc(Tp.sem, 1)

            def scores(r, i):
                b, t = divmod(i, QT)
                if t == 0:
                    pe.wait_ge(Tg.sem, Tg.at(f"kb{b}", r))
                pe.wait_ge(Tv.sem, Tv.at(f"mx{i - 1}" if i else "q", r))
                for h in range(2):
                    rows = slice(64 * h, 64 * h + 64)
                    mm(T[h][:, :], qT[rows, b, t * P:(t + 1) * P], Kbd[rows, b, 8 * h:8 * h + 8, :], stop=False)
                for h in range(2):
                    m = mm(T[h][:, :], identb[:, :], mbias[:, t, :].unsqueeze(1).to_broadcast([P, 8, KEYS]), start=False)
                m.then_inc(Tp.sem, 1)

            def turn_max(r):
                pe.wait_ge(Tv.sem, Tv.at("me", r))
                for i in range(NB * QT):
                    m = pe.transpose(Tb[0:96, i * P:(i + 1) * P], nm[:, i, :, :], identb[:, :])
                m.then_inc(Tp.sem, 1)

            def scores_t(r, b, g):
                pe.wait_ge(Ta.sem, Ta.at(("m", "e00", "e01", "e10")[2 * b + g], r))
                for i in range(2):
                    for h in range(2):
                        hp, rows = TRIO[g][h][i], slice(64 * h, 64 * h + 64)
                        mm(T[h][:, i * SEQ:(i + 1) * SEQ], Kbd[rows, b, 2 * hp:2 * hp + 2, :], qT[rows, b, :],
                           start=i == 0, stop=False, skip_group_check=True)
                for i in range(2):
                    for h in range(2):
                        o, hp = T[h][:, i * SEQ:(i + 1) * SEQ], TRIO[g][h][i]
                        mm(o, selmax[:, hp, :], nmT[:, b * SEQ:(b + 1) * SEQ], start=False, stop=False, skip_group_check=True)
                        for t in range(QT):
                            m = mm(o[:, t * P:(t + 1) * P], mbias2[:, t, :, :], identb[:, :], start=False, stop=True,
                                   skip_group_check=True)
                m.then_inc(Tp.sem, 1)

            def values(r):
                pe.wait_ge(Ta.sem, Ta.at("e11", r))
                for b in range(NB):
                    for t in range(QT):
                        for hp in range(HP):
                            m = mm(T[b][:, (t * HP + hp) * VW:(t * HP + hp + 1) * VW], E[:, b, hp, t * P:(t + 1) * P], Vbd[:, b, hp, :])
                m.then_inc(Tp.sem, 1)

            def turn_o(r):
                pe.wait_ge(Tv.sem, Tv.at("n", r))
                for i in range(NB * QT):
                    m = pe.transpose(T[0][:, i * P:(i + 1) * P], on2[:, i, :, :, :], ident[:, :])
                m.then_inc(Tp.sem, 1)

            def att_out(r):
                pe.wait_ge(Ta.sem, Ta.at("t", r))
                mm(T[1][:, :], attT[:, 3, :], oT[:, :, :]).then_inc(Tp.sem, 1)

            def slot(r, q, k, nxt, prev, tail):
                if tail:
                    if k == 0:
                        turn_o(r - 2)
                    if k == 1:
                        att_out(r - 2)
                if prev:
                    if k == 1:
                        mixer_out(r - 1)
                    if k == 2:
                        turn_c(r - 1)
                    if k == 3:
                        keys_values(r - 1)
                        att_center(r - 1)
                    if k == 4:
                        att_variance(r - 1)
                    if k == 5:
                        queries(r - 1)
                    if 6 <= k < 10:
                        scores(r - 1, k - 6)
                    if k == 10:
                        turn_max(r - 1)
                    if 11 <= k < 15:
                        scores_t(r - 1, (k - 11) // 2, (k - 11) % 2)
                    if k == 15:
                        values(r - 1)
                if nxt:
                    if k == 2:
                        turn_x(r + 1)
                    if k == 3:
                        if prev:
                            pe.wait_ge(s_x1, r)
                        center_x(r + 1, 1)
                    if k == 4:
                        variance_x(r + 1, 1)
                    if k == 5:
                        center_x(r + 1, 2)
                    if k == 6:
                        variance_x(r + 1, 2)
                    if k == 8:
                        conv(r + 1)
                    if k == 9:
                        gate_in(r + 1)
                    if k == 10:
                        x_states(r + 1, 1 - q)
                    if k == 11:
                        steps_in(r + 1)

            turn_x(0)
            for n in (1, 2):
                center_x(0, n)
                variance_x(0, n)
            conv(0)
            gate_in(0)
            x_states(0, 0)
            steps_in(0)
            spread_b(0, 0, 0)
            spread_c(0, 0, 0)

            def body(r, q, nxt, prev, tail):
                for j in range(CHUNKS):
                    more = j + 1 < CHUNKS
                    if more or nxt:
                        spread_b(r if more else r + 1, q if more else 1 - q, (j + 1) % CHUNKS)
                    sum_states(r, q, 2 * j)
                    slot(r, q, 2 * j, nxt, prev, tail)
                    if more or nxt:
                        spread_c(r if more else r + 1, q if more else 1 - q, (j + 1) % CHUNKS)
                    sum_states(r, q, 2 * j + 1)
                    slot(r, q, 2 * j + 1, nxt, prev, tail)

            rounds(pe, body, slot)

            def route_pe(r, q, e):
                if e == 0:
                    if not isinstance(r, int) or r:
                        pe.wait_ge(Fv.sem, Fv.at("b2", r - 1))
                    pe.wait_ge(s_x2in[q], 8 * (r - q) + 16)
                    mm(G[1], center[:, :], x2c[q]).then_inc(Fp.sem, 1)
                if e == 1:
                    pe.wait_ge(Fa.sem, Fa.at("sq", r))
                    mm(G[0], mean[:, :], sqt[:, :]).then_inc(Fp.sem, 1)
                if e == 2:
                    pe.wait_ge(Fv.sem, Fv.at("xf", r))
                    for t in range(NTT):
                        o = G[0][:, t * EXPERTS:(t + 1) * EXPERTS]
                        mm(o, xf[q][:, t * P:(t + 1) * P], wgs[:, :], stop=False)
                        m = mm(o, onerow[:, :], bgrow[:, :], start=False)
                    m.then_inc(Fp.sem, 1)
                    for t in range(NTT):
                        m = pe.transpose(G[1][:, t * P:(t + 1) * P], x2c[q][:, t * P:(t + 1) * P], ident[:, :])
                    m.then_inc(Fp.sem, 1)
                if e == 6:
                    pe.wait_ge(Fv.sem, Fv.at("wsel", r))
                    for t in range(NTT):
                        m = pe.transpose(G[0][0:EXPERTS, t * P:(t + 1) * P], wsel[:, q, t, :], ident[:, :])
                    m.then_inc(Fp.sem, 1)
                if e == 7:
                    pe.wait_ge(Fa.sem, Fa.at("wT", r))
                    pe.wait_ge(Fv.sem, Fv.at("x2", r))
                    for t in range(NTT):
                        m = mm(G[1][:, t * P:(t + 1) * P], wselT[:, t * P:(t + 1) * P], b2s[:, :])
                    m.then_inc(Fp.sem, 1)

            for e in range(EXPERTS):
                route_pe(0, 0, e)

            def up(r, q, e):
                for j in range(HC):
                    i = e * HC + j
                    if i >= 4 or not isinstance(r, int) or r:
                        pe.wait_ge(s_hr, r * EXPERTS * HC + i - 3)
                    mm(Hid[i % 4], w1s[:, e, j * P:(j + 1) * P], xf[q][:, :]).then_inc(s_h, 1)

            def down(r, q, e):
                pe.wait_ge(s_hr, r * EXPERTS * HC + (e + 1) * HC)
                if e >= 2 or not isinstance(r, int) or r:
                    pe.wait_ge(s_ac, (r * EXPERTS + e - 1) * NTT)
                for t in range(NTT):
                    for j in range(HC):
                        m = mm(T[e % 2][:, t * P:(t + 1) * P], hid[e % 2][:, j, t * P:(t + 1) * P], w2s[:, e, j, :],
                               start=j == 0, stop=j == HC - 1)
                m.then_inc(s_o, 1)

            up(0, 0, 0)
            pe.wait_ge(s_w2, 16)

            def expert_body(r, q, nxt):
                for e in range(EXPERTS):
                    if e + 1 < EXPERTS:
                        up(r, q, e + 1)
                    if nxt:
                        route_pe(r + 1, 1 - q, e)
                        if e + 1 == EXPERTS:
                            up(r + 1, 1 - q, 0)
                    down(r, q, e)

            expert_rounds(pe, expert_body)

        @block.scalar
        def _(act):
            A = act.activation
            act.preload_act_table_set("natural_log_exp_and_others")
            act.wait_ge(s_w, WALL)
            A(Aneg[:, :, :], alog[:, :, :], ACT.Exp).then_inc(s_prea, 1)
            for i, (src, dst, rows, cols) in enumerate(turns):
                act.wait_ge(s_tr, i + 1)
                v = T[i % 2][0:cols, 0:rows]
                if isinstance(dst, int):
                    A(wdtrT[:, dst, :], v[:, 0:DTR], ACT.Copy)
                    A(wbcT[:, dst, :, :], v[:, DTR:96].unsqueeze(1).to_broadcast([P, 3, 2 * NST]), ACT.Copy).then_inc(s_tc, 1)
                else:
                    A(dst, v, ACT.Copy).then_inc(s_tc, 1)

            def square(producer, name, r, mk, bank, to):
                act.wait_ge(producer.sem, producer.at(name, r))
                A(to[:, :], bank, ACT.Square).then_inc(mk.sem, 1)

            def inverse_root(producer, name, r, mk, ln, bank, to):
                act.wait_ge(producer.sem, producer.at(name, r))
                A(to[:, :], bank, ACT.Ln, bias=epsc[:, 0:1]).then_inc(mk.sem, 1)
                act.wait_ge(mk.sem, mk.at(ln, r))
                A(to[:, :], to[:, :], ACT.Exp, scale=-0.5).then_inc(mk.sem, 1)

            def copy_x(r):
                act.wait_ge(Ap.sem, Ap.at("tr", r))
                if not isinstance(r, int) or r:
                    act.wait_ge(Ag.sem, Ag.at("xr", r - 1))
                A(xT[:, :], M[1][:, :], ACT.Copy).then_inc(Aa.sem, 1)

            def scan_input(r):
                act.wait_ge(Av.sem, Av.at("h0a", r))
                A(hpad[:, :, TAPS - 1:], xn2[:, :].rearrange("p (b s) -> p b s", b=NB), ACT.Identity, bias=bv_[:, 0:1]).then_inc(Aa.sem, 1)

            def silus(r, q):
                for d in range(DT):
                    act.wait_ge(Ap.sem, Ap.at(f"cv{d}", r))
                    A(xh[:, q, d, :], M[d][:, :], ACT.Silu, bias=convb[:, d:d + 1]).then_inc(Aa.sem, 1)
                for d in range(DT):
                    act.wait_ge(Ap.sem, Ap.at(f"rs{d}", r))
                    A(sres[:, q, d, :], M[d][:, :], ACT.Silu).then_inc(Aa.sem, 1)

            def split(r, q, n):
                if n == 1:
                    act.wait_ge(Ap.sem, Ap.at("wx", r))
                    A(dtr[:, :], M[0][0:DTR, :], ACT.Copy).then_inc(Aa.sem, 1)
                    act.wait_ge(Ap.sem, Ap.at("wbc", r))
                    A(S[:, q, :], M[1][0:96, :], ACT.Copy).then_inc(Aa.sem, 1)
                if n == 2:
                    act.wait_ge(Av.sem, Av.at("r1", r))
                    A(S[32:64, q, :], left[32:64, :], ACT.Copy)
                    A(S[64:96, q, :], left[64:96, :], ACT.Copy).then_inc(Aa.sem, 1)
                if n == 3:
                    act.wait_ge(Av.sem, Av.at("r2", r))
                    A(S[64:96, q, :], left[64:96, :], ACT.Copy).then_inc(Aa.sem, 1)

            def log_part(r, d):
                act.wait_ge(Ap.sem, Ap.at(f"dt{d}", r))
                if not isinstance(r, int) or r:
                    act.wait_ge(Ag.sem, Ag.at(f"dt{d}", r - 1))
                A(soft[:, d, :], M[d][:, :], ACT.Abs, bias=bdt[:, d:d + 1]).then_inc(Aa.sem, 1)
                act.wait_ge(Aa.sem, Aa.at(f"az{d}", r))
                A(soft[:, d, :], soft[:, d, :], ACT.Exp, scale=-1.0).then_inc(Aa.sem, 1)
                act.wait_ge(Aa.sem, Aa.at(f"ea{d}", r))
                A(soft[:, d, :], soft[:, d, :], ACT.Ln, bias=onec[:, 0:1]).then_inc(Aa.sem, 1)

            def copy_b(r, j):
                g = r * CHUNKS + j
                for half in range(2):
                    act.wait_ge(s_bp, 2 * g + half + 1)
                    if half == 0 and (j >= 2 or not isinstance(r, int) or r):
                        act.wait_ge(s_u, 2 * g - 2)
                    A(Bs[:, j % 2, 2 * half:2 * half + 2, :], Bp[:, :, :], ACT.Copy).then_inc(s_bs, 1)

            def decays(r, q, k):
                g = r * STEPS + k
                b, c, d = step_of(k)
                if k >= 2 or not isinstance(r, int) or r:
                    act.wait_ge(s_sc, g - 1)
                if k < DT:
                    act.wait_ge(Ag.sem, Ag.at(f"dt{d}", r))
                for i in range(NC):
                    m = A(dA[:, k % 2, i, 1:SEQ], dtm[:, q, d, b * SEQ + 1:(b + 1) * SEQ], ACT.Exp,
                          scale=Aneg[:, d, c * NC + i:c * NC + i + 1])
                m.then_inc(s_ex, 1)

            def copy_c(r):
                act.wait_ge(Tp.sem, Tp.at("ctr", r))
                src = T[0][:, 0:P].rearrange("p (b k) -> p b k", b=NB)
                A(cT[:, :, :], src, ACT.Copy).then_inc(Ta.sem, 1)
                for b in range(NB):
                    m = A(cT2[:, b, :, :], src[:, b, :].unsqueeze(1).to_broadcast([P, 2, KEYS]), ACT.Copy)
                m.then_inc(Ta.sem, 1)

            def copy_kv(r):
                act.wait_ge(Tp.sem, Tp.at("kv", r))
                if not isinstance(r, int) or r:
                    act.wait_ge(Tg.sem, Tg.at("kb1", r - 1))
                A(KT[:, :, :], T[1][:, 0:P].rearrange("p (b k) -> p b k", b=NB), ACT.Identity, bias=bk[:, 0:1]).then_inc(Ta.sem, 1)
                if not isinstance(r, int) or r:
                    act.wait_ge(Tp.sem, Tp.at("o", r - 1))
                for b in range(NB):
                    v = T[1][:, (b + 1) * P:(b + 2) * P].rearrange("p (g h e) -> p g h e", g=HP, h=2)
                    for h in range(2):
                        m = A(Vbd[64 * h:64 * h + 64, b, :, h * HD:(h + 1) * HD], v[64 * h:64 * h + 64, :, h, :], ACT.Copy)
                m.then_inc(Ta.sem, 1)

            def copy_max(r):
                act.wait_ge(Tp.sem, Tp.at("m", r))
                A(nmT[:, :], Tb[0:96, 0:NB * SEQ], ACT.Copy).then_inc(Ta.sem, 1)

            def exps(r, b, g):
                act.wait_ge(Tp.sem, Tp.at(f"st{b}{g}", r))
                for h in range(2):
                    hp = TRIO[g][h][0]
                    m = A(E[:, b, hp:hp + 2, :], T[h][:, :].rearrange("p (i s) -> p i s", i=2), ACT.Exp)
                m.then_inc(Ta.sem, 1)

            def copy_o(r):
                act.wait_ge(Tp.sem, Tp.at("t", r))
                A(oT[:, :, :], T[0][:, :].rearrange("p (b s) -> p b s", b=NB), ACT.Copy).then_inc(Ta.sem, 1)

            def slot(r, q, k, nxt, prev, tail):
                if tail and k == 0:
                    copy_o(r - 2)
                if prev:
                    if k == 2:
                        copy_c(r - 1)
                    if k == 3:
                        copy_kv(r - 1)
                        square(Tp, "cen", r - 1, Ta, T[0][:, :], sqt)
                    if k == 4:
                        inverse_root(Tp, "var", r - 1, Ta, "ln", T[1][:, :], rstdt)
                    if k == 10:
                        copy_max(r - 1)
                    if 11 <= k < 15:
                        exps(r - 1, (k - 11) // 2, (k - 11) % 2)
                if nxt:
                    if k == 2:
                        copy_x(r + 1)
                    if k == 3:
                        square(Ap, "cen1", r + 1, Aa, M[0][:, :], sq)
                    if k == 4:
                        inverse_root(Ap, "var1", r + 1, Aa, "ln1", M[1][:, :], rstd)
                    if k == 5:
                        square(Ap, "cen2", r + 1, Aa, M[0][:, :], sq)
                    if k == 6:
                        inverse_root(Ap, "var2", r + 1, Aa, "ln2", M[1][:, :], rstd)
                    if k == 7:
                        scan_input(r + 1)
                    if k == 9:
                        silus(r + 1, 1 - q)
                    if 10 <= k < 13:
                        split(r + 1, 1 - q, k - 9)
                    if 12 <= k < 14:
                        log_part(r + 1, k - 12)

            act.wait_ge(s_pre, NPRE + 1)
            copy_x(0)
            for n in (1, 2):
                square(Ap, f"cen{n}", 0, Aa, M[0][:, :], sq)
                inverse_root(Ap, f"var{n}", 0, Aa, f"ln{n}", M[1][:, :], rstd)
            scan_input(0)
            silus(0, 0)
            for n in (1, 2, 3):
                split(0, 0, n)
            for d in range(DT):
                log_part(0, d)
            copy_b(0, 0)
            decays(0, 0, 0)
            decays(0, 0, 1)

            def body(r, q, nxt, prev, tail):
                for k in range(STEPS):
                    more = k + 2 < STEPS
                    if more or nxt:
                        rr, qq, kk = (r, q, k + 2) if more else (r + 1, 1 - q, k + 2 - STEPS)
                        if kk % 2 == 0:
                            copy_b(rr, kk // 2)
                        decays(rr, qq, kk)
                    slot(r, q, k, nxt, prev, tail)

            rounds(act, body, slot)

            def route_act(r, q, e):
                if e == 0:
                    square(Fp, "cen", r, Fa, G[1], sqt)
                if e == 1:
                    inverse_root(Fp, "var", r, Fa, "ln", G[0], rstdt)
                if e == 3:
                    act.wait_ge(Fv.sem, Fv.at("sb", r))
                    A(pr[:, :, :], lg[:, :, :], ACT.Exp).then_inc(Fa.sem, 1)
                if e == 4:
                    act.wait_ge(Fv.sem, Fv.at("gap", r))
                    A(wt[:, 1, :], gap[:, :], ACT.Exp).then_inc(Fa.sem, 1)
                if e == 6:
                    act.wait_ge(Fp.sem, Fp.at("wT", r))
                    A(wselT[:, :], G[0][0:EXPERTS, :], ACT.Copy).then_inc(Fa.sem, 1)

            for e in range(EXPERTS):
                route_act(0, 0, e)

            def relus(r, e):
                for j in range(HC):
                    i = e * HC + j
                    act.wait_ge(s_h, r * EXPERTS * HC + i + 1)
                    if j == 0 and (e >= 2 or not isinstance(r, int) or r):
                        act.wait_ge(s_o, r * EXPERTS + e - 1)
                    A(hid[e % 2][:, j, :], Hid[i % 4], ACT.Relu, bias=b1T[:, i:i + 1]).then_inc(s_hr, 1)

            relus(0, 0)

            def expert_body(r, q, nxt):
                for e in range(EXPERTS):
                    if e + 1 < EXPERTS:
                        relus(r, e + 1)
                    if nxt:
                        route_act(r + 1, 1 - q, e)
                        if e + 1 == EXPERTS:
                            relus(r + 1, 0)

            expert_rounds(act, expert_body)

        @block.gpsimd
        def _(pool):
            TT = pool.tensor_tensor

            def residual(r, q):
                pool.wait_ge(Av.sem, Av.at("xn", r))
                TT(xres[:, q, :], xT[:, :], xn[:, :], ALU.add).then_inc(Ag.sem, 1)

            def steps_x(r, q, d):
                pool.wait_ge(Aa.sem, Aa.at(f"L{d}", r))
                pool.wait_ge(Av.sem, Av.at(f"zp{d}", r))
                TT(dtm[:, q, d, :], zpos[:, d, :], soft[:, d, :], ALU.add).then_inc(Ag.sem, 1)
                pool.wait_ge(Ag.sem, Ag.at(f"dt{d}", r))
                TT(dtx[:, q, d, :], dtm[:, q, d, :], xh[:, q, d, :], ALU.mult).then_inc(Ag.sem, 1)

            def inputs(r, q, k):
                b, c, d = step_of(k)
                if d == 0:
                    pool.wait_ge(s_bs, 2 * (r * CHUNKS + k // 2) + 2)
                if k < DT:
                    pool.wait_ge(Ag.sem, Ag.at(f"dx{d}", r))
                if k >= 2 or not isinstance(r, int) or r:
                    pool.wait_ge(s_sc, r * STEPS + k - 1)
                TT(u[:, k % 2, :, :], Bs[:, (k // 2) % 2, :, :],
                   dtx[:, q, d, b * SEQ:(b + 1) * SEQ].unsqueeze(1).to_broadcast([P, NC, SEQ]), ALU.mult).then_inc(s_u, 1)

            def gate(r, q, b):
                for d in range(DT):
                    pool.wait_ge(s_yd, r * 4 + 2 * b + d + 1)
                    if b == 0 and d == 0 and (not isinstance(r, int) or r):
                        pool.wait_ge(s_wo, r)
                    TT(gy[:, d, b * SEQ:(b + 1) * SEQ], yd[:, d, :], sres[:, q, d, b * SEQ:(b + 1) * SEQ], ALU.mult).then_inc(s_gy, 1)

            def key_blocks(r, b):
                pool.wait_ge(Ta.sem, Ta.at("KT", r))
                TT(Kbd[:, b, :, :], KT[:, b, :].unsqueeze(1).to_broadcast([P, HEADS, KEYS]),
                   blk[:, :].unsqueeze(2).to_broadcast([P, HEADS, KEYS]), ALU.mult).then_inc(Tg.sem, 1)

            def slot(r, q, k, nxt, prev, tail):
                if k == 9 and not isinstance(r, int) or k == 9 and r < ROUNDS:
                    gate(r, q, 0)
                if prev:
                    if k == 0:
                        gate(r - 1, 1 - q, 1)
                    if 4 <= k < 6:
                        key_blocks(r - 1, k - 4)
                if nxt:
                    if k == 6:
                        residual(r + 1, 1 - q)
                    if k == 13:
                        for d in range(DT):
                            steps_x(r + 1, 1 - q, d)

            pool.wait_ge(s_w, WALL)
            residual(0, 0)
            for d in range(DT):
                steps_x(0, 0, d)
            inputs(0, 0, 0)
            inputs(0, 0, 1)

            def body(r, q, nxt, prev, tail):
                for k in range(STEPS):
                    if k + 2 < STEPS:
                        inputs(r, q, k + 2)
                    elif nxt:
                        inputs(r + 1, 1 - q, k + 2 - STEPS)
                    slot(r, q, k, nxt, prev, tail)

            rounds(pool, body, slot)

        @block.vector
        def _(v):
            v.memset(Vbd[:, :, :, :], 0.0).then_inc(s_pres, 1)
            v.wait_ge(s_pres, 1)
            for h in range(2):
                v.memset(Vbd[64 * h:64 * h + 64, :, :, 2 * HD + h:2 * HD + h + 1], 1.0)
            v.memset(hpad[:, :, 0:TAPS - 1], 0.0)
            v.memset(dA[:, :, :, 0:1], 0.0)
            v.memset(nm[:, :, :, :], 0.0)
            v.memset(epsc[:, :], EPS)
            v.memset(onec[:, :], 1.0)
            v.memset(onerow[:, :], 1.0).then_inc(s_pre, 1)
            v.wait_ge(s_w, WALL)
            for d in range(DT):
                for k in range(TAPS):
                    v.tensor_scalar(win_tap[:, d * TAPS + k, :], win_nat[:, d, :], convw[:, d, k:k + 1], None, ALU.mult).then_inc(s_pre, 1)
            n = 1 + DT * TAPS

            def nxt_(ins):
                nonlocal n
                n += 1
                ins.then_inc(s_pre, 1)
                v.wait_ge(s_pre, n)
            nxt_(v.tensor_copy(identb[:, :], ident[:, :]))
            nxt_(v.tensor_copy(sel[:, :, :], pick[:, :].unsqueeze(2).to_broadcast([96, 2 * NST, P])))
            nxt_(v.tensor_copy(selmax[:, :, :].rearrange("p g (h k) -> p (g h) k", h=2), pickmax[:, :].unsqueeze(2).to_broadcast([96, HEADS, KEYS])))
            v.wait_ge(s_prea, 1)
            nxt_(v.tensor_scalar(Aneg[:, :, :], Aneg[:, :, :], -1.0, None, ALU.mult))
            nxt_(v.tensor_scalar(keep[:, :, :], mask_i[:, :, :], 0.0, None, ALU.not_equal))
            nxt_(v.tensor_scalar(mbias[:, :, :], keep[:, :, :], -MASKED, MASKED, ALU.mult, ALU.add))
            for t in range(QT):
                nxt_(v.tensor_copy(mbias2[:, t, :, :], mbias[:, t, :].unsqueeze(1).to_broadcast([P, 2, KEYS])))
            nxt_(v.tensor_reduce(kany[:, :], keep[:, :, :], AX.X, ALU.max))
            nxt_(v.tensor_scalar(kany[:, :], kany[:, :], float(HD) ** -0.5, None, ALU.mult))
            nxt_(v.memset(kanyb[:, :, :], 1.0))
            for t in range(QT):
                nxt_(v.tensor_scalar(kanyb[:, t, :], kanyb[:, t, :], kany[:, t:t + 1], None, ALU.mult))
            assert n == NPRE
            v.wait_ge(s_tr, NTURN + 1)
            nxt_(v.tensor_copy(KA[:, :], T[0][:, 0:SEQ]))

            def normed(r, n):
                v.wait_ge(Aa.sem, Aa.at(f"rs{n}", r))
                if n == 1:
                    v.tensor_tensor(xn[:, :], M[0][:, :], rstd[:, :], ALU.mult).then_inc(Av.sem, 1)
                else:
                    v.scalar_tensor_tensor(xn2[:, :], M[0][:, :], gv[:, 0:1], rstd[:, :], ALU.mult, ALU.mult).then_inc(Av.sem, 1)

            def rest(r, q, n):
                if n == 1:
                    v.wait_ge(Aa.sem, Aa.at("S1", r))
                    v.tensor_tensor(left[:, :], M[1][0:96, :], S[:, q, :], ALU.subtract).then_inc(Av.sem, 1)
                else:
                    v.wait_ge(Aa.sem, Aa.at("S2", r))
                    v.tensor_tensor(left[64:96, :], left[64:96, :], S[64:96, q, :], ALU.subtract).then_inc(Av.sem, 1)

            def positive(r, d):
                v.wait_ge(Aa.sem, Aa.at(f"az{d}", r))
                if not isinstance(r, int) or r:
                    v.wait_ge(Ag.sem, Ag.at(f"dt{d}", r - 1))
                v.tensor_scalar(zpos[:, d, :], M[d][:, :], bdt[:, d:d + 1], 0.0, ALU.add, ALU.max).then_inc(Av.sem, 1)

            def scan(r, k):
                g = r * STEPS + k
                v.wait_ge(s_ex, g + 1)
                v.wait_ge(s_u, g + 1)
                if k >= 2 or not isinstance(r, int) or r:
                    v.wait_ge(s_pd, g - 1)
                v.tensor_tensor_scan(hst[:, k % 2].rearrange("p n s -> p (n s)"), dA[:, k % 2].rearrange("p n s -> p (n s)"),
                                     u[:, k % 2].rearrange("p n s -> p (n s)"), 0.0, ALU.mult, ALU.add).then_inc(s_sc, 1)

            def times_c(r, k):
                g = r * STEPS + k
                v.wait_ge(s_sc, g + 1)
                v.wait_ge(s_cp, r * CHUNKS + k // 2 + 1)
                if k >= 2 or not isinstance(r, int) or r:
                    v.wait_ge(s_ns, g - 1)
                v.tensor_tensor(prod[:, k % 2, :, :], hst[:, k % 2, :, :], Cp[:, :, :], ALU.mult).then_inc(s_pd, 1)

            def skip(r, q, b):
                v.wait_ge(s_ns, r * STEPS + 8 * (b + 1))
                if b or not isinstance(r, int) or r:
                    v.wait_ge(s_gy, r * 4 + 2 * b)
                for d in range(DT):
                    v.scalar_tensor_tensor(yd[:, d, :], xh[:, q, d, b * SEQ:(b + 1) * SEQ], dpar[:, d:d + 1], Y[:, d, :],
                                           ALU.mult, ALU.add).then_inc(s_yd, 1)

            def mixer_out(r, q):
                v.wait_ge(s_wo, r + 1)
                if not isinstance(r, int) or r:
                    v.wait_ge(Tv.sem, Tv.at("x2", r - 1))
                v.scalar_tensor_tensor(x1T[:, :], M[0][:, :], alph[:, 0:1], xres[:, q, :], ALU.mult, ALU.add).then_inc(s_x1, 1)

            def att_normed(r):
                v.wait_ge(Ta.sem, Ta.at("rs", r))
                v.tensor_tensor(xq[:, :], T[0][:, :], rstdt[:, :], ALU.mult).then_inc(Tv.sem, 1)

            def queries(r):
                v.wait_ge(Tp.sem, Tp.at("q", r))
                v.scalar_tensor_tensor(qT[:, :, :], T[1][:, :].rearrange("p (b s) -> p b s", b=NB), bq[:, 0:1],
                                       KA[:, :].unsqueeze(1).to_broadcast([P, NB, SEQ]), ALU.add, ALU.mult).then_inc(Tv.sem, 1)

            def maxima(r, i):
                v.wait_ge(Tp.sem, Tp.at(f"s{i}", r))
                for h in range(2):
                    m = v.tensor_reduce(mx[:, i, h * 8:h * 8 + 8], T[h][:, :].rearrange("p (h k) -> p h k", k=KEYS), AX.X, ALU.max)
                m.then_inc(Tv.sem, 1)

            def split_max(r):
                v.wait_ge(Tv.sem, Tv.at("mx3", r))
                v.tensor_scalar(nm[:, :, 0, 0:HEADS], mx[:, :, :], -1.0, None, ALU.mult).then_inc(Tv.sem, 1)
                v.wait_ge(Tv.sem, Tv.at("ma", r))
                v.scalar_tensor_tensor(mleft[:, :, :], mx[:, :, :], -1.0, nm[:, :, 0, 0:HEADS], ALU.mult, ALU.subtract).then_inc(Tv.sem, 1)
                v.wait_ge(Tv.sem, Tv.at("mb", r))
                v.tensor_copy(nm[:, :, 1, 0:HEADS], mleft[:, :, :]).then_inc(Tv.sem, 1)
                v.wait_ge(Tv.sem, Tv.at("mc", r))
                v.tensor_tensor(mleft[:, :, :], mleft[:, :, :], nm[:, :, 1, 0:HEADS], ALU.subtract).then_inc(Tv.sem, 1)
                v.wait_ge(Tv.sem, Tv.at("md", r))
                v.tensor_copy(nm[:, :, 2, 0:HEADS], mleft[:, :, :]).then_inc(Tv.sem, 1)

            def normalise(r):
                v.wait_ge(Tp.sem, Tp.at("o", r))
                o = [T[b][:, 0:QT * HP * VW].rearrange("p (g w) -> p g w", w=VW) for b in range(NB)]
                for b in range(NB):
                    m = v.reciprocal(rden[:, b, :, :], o[b][:, :, 2 * HD:VW])
                m.then_inc(Tv.sem, 1)
                v.wait_ge(Tv.sem, Tv.at("r", r))
                for b in range(NB):
                    for t in range(QT):
                        m = v.tensor_tensor(on2[:, b * QT + t, :, :, :],
                                            o[b][:, t * HP:(t + 1) * HP, 0:2 * HD].rearrange("p g (h e) -> p g h e", h=2),
                                            rden[:, b, t * HP:(t + 1) * HP, :].unsqueeze(3).to_broadcast([P, HP, 2, HD]), ALU.mult)
                m.then_inc(Tv.sem, 1)

            def att_out(r):
                v.wait_ge(Tp.sem, Tp.at("wo", r))
                v.wait_ge(s_x2, 16 * (r + 1))
                v.scalar_tensor_tensor(x2o[:, :], T[1][:, :], bo[:, 0:1], x1T[:, :], ALU.add, ALU.add).then_inc(Tv.sem, 1)

            def slot(r, q, k, nxt, prev, tail):
                if k == 8 and not isinstance(r, int) or k == 8 and r < ROUNDS:
                    skip(r, q, 0)
                if tail:
                    if k == 0:
                        normalise(r - 2)
                    if k == 1:
                        att_out(r - 2)
                if prev:
                    if k == 0:
                        skip(r - 1, 1 - q, 1)
                    if k == 2:
                        mixer_out(r - 1, 1 - q)
                    if k == 5:
                        att_normed(r - 1)
                    if k == 6:
                        queries(r - 1)
                    if 7 <= k < 11:
                        maxima(r - 1, k - 7)
                    if k == 10:
                        split_max(r - 1)
                if nxt:
                    if k == 5:
                        normed(r + 1, 1)
                    if k == 7:
                        normed(r + 1, 2)
                    if 11 <= k < 13:
                        rest(r + 1, 1 - q, k - 10)
                    if 12 <= k < 14:
                        positive(r + 1, k - 12)

            normed(0, 1)
            normed(0, 2)
            rest(0, 0, 1)
            rest(0, 0, 2)
            positive(0, 0)
            positive(0, 1)
            scan(0, 0)

            def body(r, q, nxt, prev, tail):
                for k in range(STEPS):
                    if k + 1 < STEPS:
                        scan(r, k + 1)
                    elif nxt:
                        scan(r + 1, 0)
                    times_c(r, k)
                    slot(r, q, k, nxt, prev, tail)

            rounds(v, body, slot)

            def route(r, q, e):
                def go(ins, name):
                    ins.then_inc(Fv.sem, 1)
                    v.wait_ge(Fv.sem, Fv.at(name, r))
                if e == 1:
                    v.wait_ge(Fa.sem, Fa.at("rs", r))
                    v.tensor_tensor(xf[q][:, :], G[1], rstdt[:, :], ALU.mult).then_inc(Fv.sem, 1)
                if e == 2:
                    v.wait_ge(Fp.sem, Fp.at("g", r))
                    lp = G[0][:, 0:NTT * EXPERTS].rearrange("p (t e) -> p t e", t=NTT)
                    go(v.tensor_reduce(lmax[:, :], lp, AX.X, ALU.max), "mx")
                    go(v.tensor_tensor(lg[:, :, :], lp, lmax[:, :].unsqueeze(2).to_broadcast([P, NTT, EXPERTS]), ALU.subtract), "sb")
                    v.wait_ge(Fp.sem, Fp.at("x2", r))
                    if not isinstance(r, int) or r >= 2:
                        v.wait_ge(s_out[q], 8 * (r - q))
                    go(v.tensor_copy(acc[q], G[1].rearrange("p (t d) -> p t d", t=NTT)), "x2")
                if e == 3:
                    v.wait_ge(Fa.sem, Fa.at("e", r))
                    go(v.tensor_reduce(lsum[:, :], pr[:, :, :], AX.X, ALU.add), "pe0")
                    go(v.reciprocal(lsum[:, :], lsum[:, :]), "rs")
                    go(v.tensor_tensor(pr[:, :, :], pr[:, :, :], lsum[:, :].unsqueeze(2).to_broadcast([P, NTT, EXPERTS]), ALU.mult), "pr")
                    v.memset(idle[:, 0:1], 0.0)
                    for t in range(NTT):
                        v.max(top[:, t, :], pr[:, t, :]).then_inc(Fv.sem, 1)
                    v.wait_ge(Fv.sem, Fv.at(f"t{NTT - 1}", r))
                    v.memset(idle[:, 1:2], 0.0)
                    for t in range(NTT):
                        v.max_index(topi[:, t, :], top[:, t, :], pr[:, t, :]).then_inc(Fv.sem, 1)
                    v.wait_ge(Fv.sem, Fv.at(f"i{NTT - 1}", r))
                    go(v.tensor_copy(topf[:, :, :], topi[:, :, 0:2]), "tf")
                    go(v.tensor_tensor(gap[:, :], top[:, :, 1], top[:, :, 0], ALU.subtract), "gap")
                if e == 5:
                    v.wait_ge(Fa.sem, Fa.at("ge", r))
                    go(v.tensor_scalar(wt[:, 0, :], wt[:, 1, :], 1.0, None, ALU.add), "gs")
                    go(v.reciprocal(wt[:, 0, :], wt[:, 0, :]), "w0")
                    go(v.tensor_tensor(wt[:, 1, :], wt[:, 1, :], wt[:, 0, :], ALU.mult), "w1")
                    ib = iota[:, :].unsqueeze(1).to_broadcast([P, NTT, EXPERTS])
                    for i in range(2):
                        go(v.tensor_tensor(hot[:, i, :, :], topf[:, :, i:i + 1].to_broadcast([P, NTT, EXPERTS]), ib, ALU.is_equal), f"h{i}")
                    for i in range(2):
                        go(v.tensor_tensor(hot[:, i, :, :], hot[:, i, :, :], wt[:, i, :].unsqueeze(2).to_broadcast([P, NTT, EXPERTS]), ALU.mult), f"g{i}")
                    go(v.tensor_tensor(wsel[:, q, :, :], hot[:, 0, :, :], hot[:, 1, :, :], ALU.add), "wsel")
                if e == 7:
                    v.wait_ge(Fp.sem, Fp.at("b2", r))
                    go(v.tensor_tensor(acc[q], acc[q], G[1].rearrange("p (t d) -> p t d", t=NTT), ALU.add), "b2")

            for e in range(EXPERTS):
                route(0, 0, e)

            def expert_body(r, q, nxt):
                for e in range(EXPERTS):
                    v.wait_ge(s_o, r * EXPERTS + e + 1)
                    if e:
                        v.wait_ge(s_ac, (r * EXPERTS + e) * NTT)
                    for t in range(NTT):
                        v.scalar_tensor_tensor(acc[q][:, t, :], T[e % 2][:, t * P:(t + 1) * P], wsel[:, q, t, e:e + 1], acc[q][:, t, :],
                                               ALU.mult, ALU.add).then_inc(s_ac, 1)
                    if nxt:
                        route(r + 1, 1 - q, e)

            expert_rounds(v, expert_body)


_INS = ['x', 'ctx_1024', 'mask_1x1xSxS2_ik0', 'L0_attn_ln_g', 'L0_attn_ln_b', 'L0_attn_W_in', 'L0_attn_W_x',
        'L0_attn_W_dt', 'L0_attn_b_dt', 'L0_attn_W_out', 'L0_attn_conv_w', 'L0_attn_conv_b', 'L0_attn_A_log',
        'L0_attn_D_param', 'L0_attn_alpha', 'L0_xattn_w_q', 'L0_xattn_b_q', 'L0_xattn_w_k', 'L0_xattn_b_k',
        'L0_xattn_w_v', 'L0_xattn_b_v', 'L0_xattn_w_o', 'L0_xattn_b_o', 'L0_ffn_W1', 'L0_ffn_b1', 'L0_ffn_W2',
        'L0_ffn_b2', 'L0_ffn_Wg', 'L0_ffn_bg']


def constants():
    import numpy as np
    eye = np.eye(P, dtype=np.float32)
    pick = np.tile(np.eye(2 * NST, dtype=np.float32), (3, 1))
    pickmax = np.tile(np.eye(32, HEADS, dtype=np.float32), (3, 1))
    blk = (np.arange(P)[:, None] // HD == np.arange(HEADS)[None]).astype(np.float32)
    iota = np.tile(np.arange(EXPERTS, dtype=np.float32), (P, 1))
    return {"ident": eye, "center": eye - np.float32(1.0 / D), "mean": np.full((P, P), 1.0 / D, np.float32),
            "pick": pick, "pickmax": pickmax, "blk": blk, "iota": iota}


def kernel(**inputs):
    import numpy as _np
    import concourse.bacc as _bacc
    from concourse import mybir as _mybir
    from concourse.bass_utils import run_bass_kernel_spmd as _run

    nc = _bacc.Bacc("TRN2", target_bir_lowering=False, num_devices=1)
    arrays, args = {}, []
    for name, a in [(n, inputs[n]) for n in _INS] + list(constants().items()):
        a = _np.ascontiguousarray(a)
        arrays[f"in_{name}"] = a
        args.append(nc.dram_tensor(f"in_{name}", a.shape, _mybir.dt.from_np(a.dtype), kind="ExternalInput").ap())
    args.append(nc.dram_tensor("out_0", (BATCH, SEQ, D), _mybir.dt.float32, kind="ExternalOutput").ap())
    decoder(nc, *args)
    r = _run(nc, [arrays], core_ids=[0])
    return r.results[0]["out_0"]
```

```python
import concourse.bass as bass
from concourse import mybir
from contextlib import ExitStack

ALU = mybir.AluOpType
ACT = mybir.ActivationFunctionType
BF16 = mybir.dt.bfloat16
F32 = mybir.dt.float32
I32 = mybir.dt.int32
U32 = mybir.dt.uint32
AX = mybir.AxisListType

P = 128
BATCH, SEQ, D = 16, 256, 128
DI, NST, DTR, TAPS = 256, 16, 64, 4
KEYS, HEADS, HD = 64, 16, 8
EXPERTS, HID = 8, 512
NB = 2
TOK = NB * SEQ
ROUNDS = BATCH // NB
DT = DI // P
NC = 4
CHUNKS = NB * NST // NC
STEPS = CHUNKS * DT
RING = 4
LAG = 2
PIECES = 4
SPREADS = 3
HP = HEADS // 2
GW = 32
QT = SEQ // P
HC = HID // P
EPS = 1e-5
EXP_LN = "natural_log_exp_and_others"
MASKED = -1e9


class Marks:

    def __init__(self, sem, names):
        self.sem, self.names = sem, names.split()

    def at(self, name, r):
        return r * len(self.names) + self.names.index(name) + 1

    def all(self, r):
        return (r + 1) * len(self.names)


def decoder(nc, x, ctx_in, mask, ln_g, ln_b, W_in, W_x, W_dt, b_dt, W_out, conv_w, conv_b, A_log, D_param,
            alpha, w_q, b_q, w_k, b_k, w_v, b_v, w_o, b_o, W1, b1, W2, b2, Wg, bg,
            c_ident, c_center, c_mean, c_pick, c_pickmax, c_blk, c_iota, out):
    with ExitStack() as es:
        def sb(name, shape, dt=F32):
            return es.enter_context(nc.sbuf_tensor(name, shape, dt))

        def ps(name, shape, dt=F32):
            return es.enter_context(nc.psum_tensor(name, shape, dt))

        def sem(name):
            return es.enter_context(nc.semaphore(name))

        ident = sb("ident", [P, P])
        identb = sb("identb", [P, P], BF16)
        center = sb("center", [P, P])
        mean = sb("mean", [P, P])
        sel = sb("sel", [96, 2 * NST, P], BF16)
        selmax = sb("selmax", [96, HP, P], BF16)
        pick = sb("pick", [96, 2 * NST])
        pickmax = sb("pickmax", [96, HEADS])
        blk = sb("blk", [P, HEADS])
        iota = sb("iota", [P, EXPERTS])
        E = sb("E", [P, NB, HP, SEQ])
        spare = E[:, :, :, :].rearrange("p b g s -> p (b g s)")
        took = [0]

        def borrow(rows, cols):
            took[0] += cols
            return spare[0:rows, took[0] - cols:took[0]]

        win_nat = borrow(P, 4 * D).rearrange("p (n d) -> p n d", n=4)
        wx_nat = borrow(96, DI)
        wdt_nat = borrow(P, DT * DTR).rearrange("p (n r) -> p n r", n=DT)
        wout_nat = borrow(P, DI)
        att_nat = borrow(P, 4 * D).rearrange("p (n d) -> p n d", n=4)
        b1_nat = borrow(EXPERTS * HC, P)
        winT = sb("winT", [P, DT * TAPS + DT, P])
        wdtrT = sb("wdtrT", [P, DT, DTR])
        wbcT = sb("wbcT", [P, DT, 3, 2 * NST])
        wdtT = sb("wdtT", [DTR, DT, P])
        woutT = sb("woutT", [P, DT, P])
        attT = sb("attT", [P, 4, P])
        b1T = sb("b1T", [P, EXPERTS * HC])
        win_tap = borrow(P, DT * TAPS * D).rearrange("p (i d) -> p i d", d=D)
        lng = sb("lng", [P, 1])
        lnb = sb("lnb", [P, 1])
        convw = sb("convw", [P, DT, TAPS])
        convb = sb("convb", [P, DT])
        bdt = sb("bdt", [P, DT])
        alog = sb("alog", [P, DT, NST])
        Aneg = sb("Aneg", [P, DT, NST])
        dpar = sb("dpar", [P, DT])
        alph = sb("alph", [P, 1])
        bq = sb("bq", [P, 1])
        bk = sb("bk", [P, 1])
        bo = sb("bo", [P, 1])
        bv = sb("bv", [P, 1])
        epsc = sb("epsc", [P, 1])
        idle = sb("idle", [P, 2])
        onec = sb("onec", [P, 1])
        mask_i = sb("mask_i", [P, QT, KEYS], I32)
        keep = sb("keep", [P, QT, KEYS])
        kany = sb("kany", [P, QT])
        kanyb = borrow(P, QT * P).rearrange("p (t m) -> p t m", t=QT)
        KA = sb("KA", [P, SEQ])
        mbias = sb("mbias", [P, QT, KEYS], BF16)
        mbias2 = sb("mbias2", [P, QT, 2, KEYS], BF16)
        b2s = sb("b2s", [EXPERTS, D])
        wgs = sb("wgs", [P, EXPERTS])
        bgs = sb("bgs", [P, EXPERTS])

        xin = sb("xin", [P, TOK // P, D])
        xT = sb("xT", [P, TOK])
        sq = sb("sq", [P, TOK])
        rstd = sb("rstd", [P, TOK])
        xn = sb("xn", [P, TOK])
        xn2 = sb("xn2", [P, TOK])
        hpad = sb("hpad", [P, NB, TAPS - 1 + SEQ])
        xh = sb("xh", [P, 2, DT, TOK])
        sres = sb("sres", [P, 2, DT, TOK])
        dtr = sb("dtr", [DTR, TOK])
        S = sb("S", [96, 2, TOK], BF16)
        left = sq[0:96, :]
        soft = sb("soft", [P, DT, TOK])
        dtm = sb("dtm", [P, 2, DT, TOK])
        dtx = sb("dtx", [P, 2, DT, TOK])
        xres = sb("xres", [P, 2, TOK])

        dA = sb("dA", [P, RING, NC, SEQ])
        u = sb("u", [P, RING, NC, SEQ])
        prod = sb("prod", [P, RING, NC, SEQ])
        hst = sb("hst", [P, 2, NC, SEQ])
        Bs = sb("Bs", [P, 2, NC, SEQ])
        Cs = sb("Cs", [P, 2, NC, SEQ])
        yd = sb("yd", [P, DT, SEQ])
        gy = sb("gy", [P, DT, TOK])
        x1T = sb("x1T", [P, TOK])

        cin = sb("cin", [P, D])
        cT = sb("cT", [P, NB, KEYS])
        cT2 = sb("cT2", [P, NB, 2, KEYS])
        KT = sb("KT", [P, NB, KEYS])
        Kbd = sb("Kbd", [P, NB, HEADS, KEYS])
        Vg = sb("Vg", [P, NB, HP, GW])
        ones = sb("ones", [P, 2, GW])
        qT = sb("qT", [P, NB, SEQ])
        sqt = sb("sqt", [P, TOK])
        xq = sqt
        rstdt = sb("rstdt", [P, TOK])
        mx = sb("mx", [P, NB * QT, HEADS])
        mleft = sb("mleft", [P, NB * QT, HEADS])
        nm = sb("nm", [P, NB * QT, 3, 32], BF16)
        nmT = sb("nmT", [96, NB * SEQ], BF16)
        rden = rstdt
        oT = sb("oT", [P, TOK])
        x2o = sb("x2o", [P, TOK])
        x2d = nc.dram_tensor("x2d", (ROUNDS, P, TOK), F32).ap()

        x2c = [xin[:, :, :].rearrange("p t d -> p (t d)"), xT[:, :]]
        xf = [xn2, xn]
        w2s = u[:, :, :, :].rearrange("p a n s -> p (a n s)").rearrange("p (e j c) -> p e j c", e=EXPERTS, j=HC)
        w1s = dA[:, :, :, :].rearrange("p a n s -> p (a n s)").rearrange("p (e h) -> p e h", e=EXPERTS)
        lg = sb("lg", [P, TOK // P, EXPERTS])
        pr = sb("pr", [P, TOK // P, EXPERTS])
        lmax = sb("lmax", [P, TOK // P])
        lsum = sb("lsum", [P, TOK // P])
        top = sb("top", [P, TOK // P, 8])
        topi = sb("topi", [P, TOK // P, 8], U32)
        topf = sb("topf", [P, TOK // P, 2])
        gap = sb("gap", [P, TOK // P])
        wt = sb("wt", [P, 2, TOK // P])
        hot = sb("hot", [P, 2, TOK // P, EXPERTS])
        wsel = sb("wsel", [P, 2, TOK // P, EXPERTS])
        wselT = dtr[0:EXPERTS, :]
        hid = [t[:, 0:2, :, :].rearrange("p a n s -> p (a n s)").rearrange("p (j t) -> p j t", j=HC) for t in (hst, prod)]
        acc = [xres[:, i, :].rearrange("p (t d) -> p t d", d=D) for i in range(2)]

        Rp = ps("Rp", [P, SPREADS, 2, SEQ])
        Y = ps("Y", [P, DT, SEQ])
        M = [ps("M0", [P, 512]), ps("M1", [P, 512])]
        T = [ps("T0", [P, 512]), ps("T1", [P, 512])]

        Hid = [M[0][:, :], M[1][:, :]] + [Rp[:, i, :, :].rearrange("p n s -> p (n s)") for i in range(2)]
        G = [t.rearrange("p n s -> p (n s)") for t in (Rp[:, 2, :, :], Y[:, :, :])]
        Ts = [T[0][:, :], T[1][:, :]]
        G_first = Hid_first = Hid[0:2]
        Ts_first = Hid[2:4]
        Tb = T[0][:, :].bitcast(BF16)

        s_first = sem("s_first")
        s_w = sem("s_w")
        s_tr = sem("s_tr")
        s_tc = sem("s_tc")
        s_pre = sem("s_pre")
        s_prea = sem("s_prea")
        s_pres = sem("s_pres")
        s_w1 = sem("s_w1")
        s_w2 = sem("s_w2")
        s_x = sem("s_x")
        s_c = sem("s_c")
        Ap = Marks(sem("Ap"), "tr cen1 var1 cen2 var2 cv0 cv1 rs0 rs1 wx wbc dt0 dt1")
        Aa = Marks(sem("Aa"), "xT sq1 ln1 rs1 sq2 ln2 rs2 h0 xh0 xh1 sr0 sr1 dtr S1 S2 az0 ea0 L0 S3 az1 ea1 L1")
        Av = Marks(sem("Av"), "xn h0a r1 zp0 r2 zp1")
        Ag = Marks(sem("Ag"), "xr dt0 dx0 dt1 dx1")
        s_sp = sem("s_sp")
        s_cp = sem("s_cp")
        s_ex = sem("s_ex")
        s_u = sem("s_u")
        s_sc = sem("s_sc")
        s_pd = sem("s_pd")
        s_fd = sem("s_fd")
        s_ns = sem("s_ns")
        s_yd = sem("s_yd")
        s_gy = sem("s_gy")
        s_wo = sem("s_wo")
        s_x1 = sem("s_x1")
        Tp = Marks(sem("Tp"), "ctr cen kv var q " + " ".join(f"s{i}a s{i}b" for i in range(NB * QT)) + " m st00 st01 st10 st11 o wo")
        Ta = Marks(sem("Ta"), "cT cT2 sq ln rs m e00 e01 e10 e11 ld rd")
        Tv = Marks(sem("Tv"), "KT v xq q " + " ".join(f"mx{i}a mx{i}b" for i in range(NB * QT)) + " ma mb mc md me n x2")
        Tg = Marks(sem("Tg"), "kb0 kb1")
        Fp = Marks(sem("Fp"), "cen var g x2 wT b2")
        Fa = Marks(sem("Fa"), "sq ln rs e ge wT")
        s_h = sem("s_h")
        s_hr = sem("s_hr")
        s_o = sem("s_o")
        s_ac = sem("s_ac")
        Fv = Marks(sem("Fv"), "xf lg mx sb x2 pe0 rs pr " + " ".join(f"{w}{t}" for w in "ti" for t in range(TOK // P))
                   + " tf gap gs w0 w1 h0 h1 g0 g1 wsel b2")
        s_x2 = sem("s_x2")
        s_x2in = [sem(f"s_x2in{q}") for q in range(2)]
        s_out = [sem(f"s_out{q}") for q in range(2)]

        xd = x.rearrange("b s d -> (b s) d")
        od = out.rearrange("b s d -> (b s) d")
        cd = ctx_in.rearrange("b k d -> (b k) d")

        first_loads = [
            (ident[:, :], c_ident), (center[:, :], c_center), (mean[:, :], c_mean),
            (lng[:, :], ln_g.rearrange("(p o) -> p o", o=1)), (lnb[:, :], ln_b.rearrange("(p o) -> p o", o=1)),
        ]
        FIRST = 16 * len(first_loads)
        loads = [
            (win_nat[:, :, :], W_in.rearrange("(n p) d -> p n d", p=P)),
            (convw[:, :, :], conv_w.rearrange("(n p) o k -> p n (o k)", p=P)),
            (wx_nat[:, :], W_x), (wdt_nat[:, :, :], W_dt.rearrange("(n p) r -> p n r", p=P)),
            (wout_nat[:, :], W_out),
            (convb[:, :], conv_b.rearrange("(n p) -> p n", p=P)), (bdt[:, :], b_dt.rearrange("(n p) -> p n", p=P)),
            (alog[:, :, :], A_log.rearrange("(n p) s -> p n s", p=P)),
            (dpar[:, :], D_param.rearrange("(n p) -> p n", p=P)),
            (alph[:, :], alpha.partition_broadcast(P)),
            (pick[:, :], c_pick), (pickmax[:, :], c_pickmax), (blk[:, :], c_blk), (iota[:, :], c_iota),
            (att_nat[:, 0, :], w_q), (att_nat[:, 1, :], w_k), (att_nat[:, 2, :], w_v), (att_nat[:, 3, :], w_o),
            (bq[:, :], b_q.rearrange("(p o) -> p o", o=1)), (bk[:, :], b_k.rearrange("(p o) -> p o", o=1)),
            (bo[:, :], b_o.rearrange("(p o) -> p o", o=1)), (bv[:, :], b_v.rearrange("(p o) -> p o", o=1)),
            (mask_i[:, :, :], mask.rearrange("a b (t p) k -> p (a b t) k", p=P)),
            (b1_nat[:, :], b1.rearrange("e (j p) -> (e j) p", p=P)), (b2s[:, :], b2), (wgs[:, :], Wg),
            (bgs[:, :], bg.partition_broadcast(P)),
        ]
        WALL = 16 * len(loads)

        turns = [(win_tap[:, i:i + 4, :], winT[:, i:i + 4, :], P, P) for i in range(0, DT * TAPS, 4)]
        turns += [(win_nat[:, DT:2 * DT, :], winT[:, DT * TAPS:DT * TAPS + DT, :], P, P)]
        turns += [(wx_nat[:, i * P:(i + 1) * P].unsqueeze(1), i, 96, P) for i in range(DT)]
        turns += [(wdt_nat[:, :, :], wdtT[:, :, :], P, DTR)]
        turns += [(wout_nat.rearrange("p (n d) -> p n d", n=DT), woutT[:, :, :], P, P)]
        turns += [(att_nat[:, :, :], attT[:, :, :], P, P)]
        turns += [(b1_nat.unsqueeze(1), b1T[:, :].unsqueeze(1), EXPERTS * HC, P)]
        NTURN = len(turns)
        MIXER = DT * TAPS // 4 + 2 + DT
        NPRE = 1 + DT * TAPS + 13

        block = es.enter_context(nc.Block())

        def rounds(eng, body, drain):
            body(0, 0, ln=True, nxt=True, prev=False, tail=False)
            body(1, 1, ln=True, nxt=True, prev=True, tail=False)
            with eng.Fori(2, ROUNDS - 2, 2) as r:
                body(r, 0, ln=True, nxt=True, prev=True, tail=True)
                body(r + 1, 1, ln=True, nxt=True, prev=True, tail=True)
            body(ROUNDS - 2, 0, ln=False, nxt=True, prev=True, tail=True)
            body(ROUNDS - 1, 1, ln=False, nxt=False, prev=True, tail=True)
            for n in range(DRAIN):
                drain(n)

        DRAIN = STEPS + 5
        FIRST_UNIT = DRAIN - 2 * EXPERTS - 1

        def drain_slot(n):
            return dict(r=ROUNDS + n // STEPS, q=n // STEPS, k=n % STEPS, ln=False, nxt=False, prev=n < STEPS, tail=True)

        def is_last(r):
            return isinstance(r, int) and r == ROUNDS - 1

        def expert_rounds(eng, body):
            with eng.Fori(1, ROUNDS - 1, 2) as r:
                body(r, 1, nxt=True)
                body(r + 1, 0, nxt=True)
            body(ROUNDS - 1, 1, nxt=False)

        NTT = TOK // P
        TRIO = ((0, 1), (4, 5)), ((2, 3), (6, 7))

        def later(r, i=0, first=1):
            return not isinstance(r, int) or r > 0 or i >= first

        def step_of(k):
            return k // (STEPS // NB), (k // DT) % (NST // NC), k % DT

        @block.sync
        def _(sp):
            for dst, src in first_loads:
                sp.dma_start(dst, src, allow_slow_non_contiguous=True).then_inc(s_first, 16)

            def load_x(r):
                if not isinstance(r, int) or r:
                    sp.wait_ge(Ap.sem, Ap.at("tr", r - 1))
                sp.dma_start(xin[:, :, :], xd[bass.ds(r * TOK, TOK), :].rearrange("(n p) d -> p n d", p=P)).then_inc(s_x, 16)

            def load_c(r):
                if not isinstance(r, int) or r:
                    sp.wait_ge(Tp.sem, Tp.at("ctr", r - 1))
                sp.dma_start(cin[:, :], cd[bass.ds(r * NB * KEYS, NB * KEYS), :]).then_inc(s_c, 16)

            def store_x2(r):
                sp.wait_ge(Tv.sem, Tv.all(r))
                sp.dma_start(x2d[r, :, :] if isinstance(r, int) else x2d[bass.ds(r, 1), :, :].rearrange("o p t -> p (o t)"), x2o[:, :]).then_inc(s_x2, 16)

            def load_x2(r, q):
                if not isinstance(r, int) or r >= 2:
                    sp.wait_ge(Fp.sem, Fp.at("x2", r - 2))
                src = x2d[r, :, :] if isinstance(r, int) else x2d[bass.ds(r, 1), :, :].rearrange("o p t -> p (o t)")
                sp.dma_start(x2c[q], src).then_inc(s_x2in[q], 16)

            def store(r, q):
                sp.wait_ge(s_ac, (r + 1) * EXPERTS * NTT)
                sp.dma_start(od[bass.ds(r * TOK, TOK), :].rearrange("(n p) d -> p n d", p=P), acc[q]).then_inc(s_out[q], 16)

            sp.sem_inc(s_x2, 16)
            load_x(0)
            for dst, src in loads:
                sp.dma_start(dst, src, allow_slow_non_contiguous=True).then_inc(s_w, 16)
            load_c(0)
            load_x(1)
            load_x(2)
            load_x(3)
            load_c(1)
            with sp.Fori(4, ROUNDS) as r:
                load_c(r - 2)
                store_x2(r - 4)
                load_x(r)
            load_c(ROUNDS - 2)
            store_x2(ROUNDS - 4)
            sp.wait_ge(Ag.sem, Ag.at("xr", ROUNDS - 1))
            sp.wait_ge(Ap.sem, Ap.at("tr", ROUNDS - 1))
            sp.wait_ge(s_x2, 16 * 3)
            load_x2(0, 0)
            load_x2(1, 1)
            load_c(ROUNDS - 1)
            store_x2(ROUNDS - 3)
            sp.wait_ge(s_sc, ROUNDS * STEPS)
            sp.dma_start(w1s, W1.rearrange("e c h -> c e h")).then_inc(s_w1, 16)
            sp.dma_start(w2s, W2.rearrange("e (j p) c -> p e j c", p=P)).then_inc(s_w2, 16)
            store_x2(ROUNDS - 2)
            load_x2(2, 0)
            store_x2(ROUNDS - 1)
            sp.wait_ge(s_x2, 16 * (ROUNDS + 1))
            store(0, 0)

            with sp.Fori(1, ROUNDS - 3, 2) as r:
                for i in range(2):
                    load_x2(r + 2 + i, (1, 0)[i])
                    store(r + i, (1, 0)[i])
            load_x2(ROUNDS - 1, 1)
            store(ROUNDS - 3, 1)
            store(ROUNDS - 2, 0)
            store(ROUNDS - 1, 1)
            for q in range(2):
                sp.wait_ge(s_out[q], 8 * ROUNDS)

        @block.tensor
        def _(pe):
            def mm(o, l, r_, start=True, stop=True, **kw):
                return pe.matmul(o, l, r_, start=start, stop=stop, **kw)

            def turn_x(r):
                pe.wait_ge(s_x, 16 * (r + 1))
                if later(r):
                    pe.wait_ge(Av.sem, Av.all(r - 1))
                for t in range(NTT):
                    m = pe.transpose(M[1][:, t * P:(t + 1) * P], xin[:, t, :], ident[:, :])
                m.then_inc(Ap.sem, 1)

            def center_x(r, n):
                if n == 1:
                    pe.wait_ge(Aa.sem, Aa.at("xT", r))
                    mm(M[0][:, :], center[:, :], xT[:, :]).then_inc(Ap.sem, 1)
                else:
                    pe.wait_ge(Av.sem, Av.at("xn", r))
                    mm(M[0][:, :], center[:, :], xn[:, :]).then_inc(Ap.sem, 1)

            def variance_x(r, n):
                pe.wait_ge(Aa.sem, Aa.at(f"sq{n}", r))
                mm(M[1][:, :], mean[:, :], sq[:, :]).then_inc(Ap.sem, 1)

            def conv(r, d):
                pe.wait_ge(Aa.sem, Aa.at("h0", r))
                for k in range(TAPS):
                    m = mm(M[d][:, :], winT[:, d * TAPS + k, :], hpad[:, :, k:k + SEQ], start=k == 0, stop=k == TAPS - 1)
                m.then_inc(Ap.sem, 1)

            def gate_in(r):
                for d in range(DT):
                    pe.wait_ge(Aa.sem, Aa.at(f"xh{d}", r))
                    mm(M[d][:, :], winT[:, DT * TAPS + d, :], hpad[:, :, TAPS - 1:TAPS - 1 + SEQ]).then_inc(Ap.sem, 1)

            def x_steps(r, q):
                pe.wait_ge(Aa.sem, Aa.at("sr0", r))
                for d in range(DT):
                    m = mm(M[0][0:DTR, :], wdtrT[:, d, :], xh[:, q, d, :], start=d == 0, stop=d == DT - 1)
                m.then_inc(Ap.sem, 1)

            def x_states(r, q):
                pe.wait_ge(Aa.sem, Aa.at("sr1", r))
                for d in range(DT):
                    m = mm(M[1][0:96, :], wbcT[:, d, :, :], xh[:, q, d, :], start=d == 0, stop=d == DT - 1)
                m.then_inc(Ap.sem, 1)

            def steps_in(r, d):
                if d == 0:
                    pe.wait_ge(Aa.sem, Aa.at("dtr", r))
                else:
                    pe.wait_ge(Av.sem, Av.at("r1", r))
                mm(M[d][:, :], wdtT[:, d, :], dtr[:, :]).then_inc(Ap.sem, 1)

            def spread(r, q, j, of):
                b, c = divmod(j, NST // NC)
                if j == 0 and of == 0:
                    pe.wait_ge(Aa.sem, Aa.at("S3", r))
                for half in range(2):
                    i = j * PIECES + of * 2 + half
                    if later(r, i, SPREADS):
                        pe.wait_ge(s_cp, r * CHUNKS * PIECES + (i - SPREADS + 1 if i >= SPREADS else i - CHUNKS * PIECES % SPREADS + 1))
                    for n in range(2):
                        m = mm(Rp[:, i % SPREADS, n, :], sel[:, of * NST + c * NC + 2 * half + n, :], S[:, q, b * SEQ:(b + 1) * SEQ])
                    m.then_inc(s_sp, 1)

            def sum_states(r, q, k):
                b, c, d = step_of(k)
                if c == 0 and d == 0 and (b or not isinstance(r, int) or r):
                    pe.wait_ge(s_yd, r * 4 + 2 * b)
                pe.wait_ge(s_fd, r * STEPS + k + 1)
                for i in range(NC // 2):
                    m = mm(Y[:, d, :], ident[:, :], prod[:, k % RING, i, :], start=c == 0 and d == 0 and i == 0,
                           stop=c == NST // NC - 1 and i == NC // 2 - 1, skip_group_check=True)
                m.then_inc(s_ns, 1)

            def mixer_out(r):
                pe.wait_ge(s_gy, 4 * (r + 1))
                for d in range(DT):
                    m = mm(T[0][:, :], woutT[:, d, :], gy[:, d, :], start=d == 0, stop=d == DT - 1)
                m.then_inc(s_wo, 1)

            def turn_c(r):
                pe.wait_ge(s_c, 16 * (r + 1))
                if later(r):
                    pe.wait_ge(Tv.sem, Tv.at("x2", r - 1))
                pe.transpose(T[1][:, 0:P], cin[:, :], ident[:, :]).then_inc(Tp.sem, 1)

            def keys_values(r):
                pe.wait_ge(Ta.sem, Ta.at("cT2", r))
                mm(T[1][:, 0:P], attT[:, 1, :], cT[:, :, :])
                for b in range(NB):
                    m = mm(T[1][:, (b + 1) * P:(b + 2) * P], cT2[:, b, :, :], attT[:, 2, :])
                m.then_inc(Tp.sem, 1)

            def att_center(r):
                pe.wait_ge(s_x1, r + 1)
                mm(T[0][:, :], center[:, :], x1T[:, :]).then_inc(Tp.sem, 1)

            def att_variance(r):
                pe.wait_ge(Ta.sem, Ta.at("sq", r))
                pe.wait_ge(Tv.sem, Tv.at("v", r))
                mm(T[1][:, :], mean[:, :], sqt[:, :]).then_inc(Tp.sem, 1)

            def queries(r):
                pe.wait_ge(Tv.sem, Tv.at("xq", r))
                mm(T[1][:, :], attT[:, 0, :], xq[:, :]).then_inc(Tp.sem, 1)

            def scores(r, i):
                b, t = divmod(i, QT)
                if t == 0:
                    pe.wait_ge(Tg.sem, Tg.at(f"kb{b}", r))
                for h in range(2):
                    if i:
                        pe.wait_ge(Tv.sem, Tv.at(f"mx{i - 1}{'ab'[h]}", r))
                    elif h == 0:
                        pe.wait_ge(Tv.sem, Tv.at("q", r))
                    rows = slice(64 * h, 64 * h + 64)
                    mm(T[h][:, :], qT[rows, b, t * P:(t + 1) * P], Kbd[rows, b, 8 * h:8 * h + 8, :], stop=False)
                for h in range(2):
                    mm(T[h][:, :], identb[:, :], mbias[:, t, :].unsqueeze(1).to_broadcast([P, 8, KEYS]), start=False).then_inc(Tp.sem, 1)

            def turn_max(r):
                pe.wait_ge(Tv.sem, Tv.at("me", r))
                for i in range(NB * QT):
                    m = pe.transpose(Tb[0:96, i * P:(i + 1) * P], nm[:, i, :, :], identb[:, :])
                m.then_inc(Tp.sem, 1)

            def scores_t(r, b, g):
                pe.wait_ge(Ta.sem, Ta.at(("m", "e00", "e01", "e10")[2 * b + g], r))
                for i in range(2):
                    for h in range(2):
                        hp, rows = TRIO[g][h][i], slice(64 * h, 64 * h + 64)
                        mm(T[h][:, i * SEQ:(i + 1) * SEQ], Kbd[rows, b, 2 * hp:2 * hp + 2, :], qT[rows, b, :],
                           start=i == 0, stop=False, skip_group_check=True)
                for i in range(2):
                    for h in range(2):
                        o, hp = T[h][:, i * SEQ:(i + 1) * SEQ], TRIO[g][h][i]
                        mm(o, selmax[:, hp, :], nmT[:, b * SEQ:(b + 1) * SEQ], start=False, stop=False, skip_group_check=True)
                        for t in range(QT):
                            m = mm(o[:, t * P:(t + 1) * P], mbias2[:, t, :, :], identb[:, :], start=False, stop=True,
                                   skip_group_check=True)
                m.then_inc(Tp.sem, 1)

            def values(r):
                pe.wait_ge(Ta.sem, Ta.at("e11", r))
                for b in range(NB):
                    for p in range(2):
                        for to, w in ((T[0], Vg[:, b, :, :]), (T[1], None)):
                            for j in range(P // GW):
                                hp = 2 * j + p
                                m = mm(to[j * GW:(j + 1) * GW, b * SEQ:(b + 1) * SEQ], ones[:, p, :] if w is None else w[:, hp, :],
                                       E[:, b, hp, :], start=p == 0, stop=p == 1, skip_group_check=True)
                m.then_inc(Tp.sem, 1)

            def att_out(r):
                pe.wait_ge(Tv.sem, Tv.at("n", r))
                mm(T[1][:, :], attT[:, 3, :], oT[:, :]).then_inc(Tp.sem, 1)

            def route_pe(r, q, e, G=G):
                if e == 0:
                    if later(r):
                        pe.wait_ge(Fv.sem, Fv.at("b2", r - 1))
                    pe.wait_ge(s_x2in[q], 8 * (r - q) + 16)
                    mm(G[1], center[:, :], x2c[q]).then_inc(Fp.sem, 1)
                if e == 1:
                    pe.wait_ge(Fa.sem, Fa.at("sq", r))
                    mm(G[0], mean[:, :], sq[:, :]).then_inc(Fp.sem, 1)
                if e == 2:
                    pe.wait_ge(Fv.sem, Fv.at("xf", r))
                    for t in range(NTT):
                        m = mm(G[0][:, t * EXPERTS:(t + 1) * EXPERTS], xf[q][:, t * P:(t + 1) * P], wgs[:, :])
                    m.then_inc(Fp.sem, 1)
                    for t in range(NTT):
                        m = pe.transpose(G[1][:, t * P:(t + 1) * P], x2c[q][:, t * P:(t + 1) * P], ident[:, :])
                    m.then_inc(Fp.sem, 1)
                if e == 6:
                    pe.wait_ge(Fv.sem, Fv.at("wsel", r))
                    for t in range(NTT):
                        m = pe.transpose(G[0][0:EXPERTS, t * P:(t + 1) * P], wsel[:, q, t, :], ident[:, :])
                    m.then_inc(Fp.sem, 1)
                if e == 7:
                    pe.wait_ge(Fa.sem, Fa.at("wT", r))
                    pe.wait_ge(Fv.sem, Fv.at("x2", r))
                    for t in range(NTT):
                        m = mm(G[1][:, t * P:(t + 1) * P], wselT[:, t * P:(t + 1) * P], b2s[:, :])
                    m.then_inc(Fp.sem, 1)

            def up(r, q, e, Hid=Hid):
                for j in range(HC):
                    i = e * HC + j
                    if later(r, i, len(Hid)):
                        pe.wait_ge(s_hr, r * EXPERTS * HC + i - len(Hid) + 1)
                    mm(Hid[i % len(Hid)], w1s[:, e, j * P:(j + 1) * P], xf[q][:, :]).then_inc(s_h, 1)

            def down(r, q, e, Ts=Ts):
                pe.wait_ge(s_hr, r * EXPERTS * HC + (e + 1) * HC)
                if e >= 2 or not isinstance(r, int) or r:
                    pe.wait_ge(s_ac, (r * EXPERTS + e - 1) * NTT)
                for t in range(NTT):
                    for j in range(HC):
                        m = mm(Ts[e % 2][:, t * P:(t + 1) * P], hid[e % 2][:, j, t * P:(t + 1) * P], w2s[:, e, j, :],
                               start=j == 0, stop=j == HC - 1)
                m.then_inc(s_o, 1)

            def slot(r, q, k, ln, nxt, prev, tail):
                if tail:
                    if k < 2:
                        scores_t(r - 2, 1, k)
                    if k == 2:
                        values(r - 2)
                    if k == 4:
                        att_out(r - 2)
                if prev:
                    if k == 4:
                        mixer_out(r - 1)
                    if k == 5:
                        turn_c(r - 1)
                        att_center(r - 1)
                    if k == 6:
                        keys_values(r - 1)
                    if k == 7:
                        att_variance(r - 1)
                    if 9 <= k < 13:
                        scores(r - 1, k - 9)
                    if k == 13:
                        turn_max(r - 1)
                    if k >= 14:
                        scores_t(r - 1, 0, k - 14)
                if nxt and k == 8:
                    x_states(r + 1, 1 - q)
                if prev and k == 8:
                    queries(r - 1)
                if nxt:
                    if k == 0:
                        variance_x(r + 1, 2)
                    if k == 3:
                        conv(r + 1, 0)
                    if k == 5:
                        conv(r + 1, 1)
                    if k == 7:
                        x_steps(r + 1, 1 - q)
                    if k == 8:
                        steps_in(r + 1, 0)
                    if k == 10:
                        steps_in(r + 1, 1)
                if ln:
                    if k == 12:
                        turn_x(r + 2)
                    if k == 13:
                        center_x(r + 2, 1)
                    if k == 14:
                        variance_x(r + 2, 1)
                    if k == 15:
                        center_x(r + 2, 2)
                if is_last(r):
                    if k == 0:
                        pe.wait_ge(Aa.sem, Aa.all(r))
                        pe.wait_ge(Av.sem, Av.all(r))
                    if k % 2:
                        route_pe(0, 0, k // 2, G_first)

            pe.wait_ge(s_first, FIRST)
            turn_x(0)
            for n in (1, 2):
                center_x(0, n)
                variance_x(0, n)
            pe.wait_ge(s_w, WALL)
            pe.wait_ge(s_pre, 1 + DT * TAPS)

            def turn_weights(first, last):
                for i in range(first, last):
                    src, _, rows, cols = turns[i]
                    if i >= 2:
                        pe.wait_ge(s_tc, i - 1)
                    for n in range(src.shape[1]):
                        m = pe.transpose(T[i % 2][0:cols, n * rows:(n + 1) * rows], src[:, n, :], ident[0:rows, 0:rows])
                    m.then_inc(s_tr, 1)
                pe.wait_ge(s_tc, last)

            turn_weights(0, MIXER)
            conv(0, 0)
            conv(0, 1)
            gate_in(0)
            x_steps(0, 0)
            x_states(0, 0)
            steps_in(0, 0)
            steps_in(0, 1)
            pe.wait_ge(s_pre, NPRE)
            spread(0, 0, 0, 0)
            spread(0, 0, 0, 1)
            turn_x(1)
            spread(0, 0, 1, 0)
            center_x(1, 1)
            turn_weights(MIXER, NTURN)
            variance_x(1, 1)
            for t in range(QT):
                mm(T[0][:, t * P:(t + 1) * P], kanyb[:, t, :], ident[:, :])
            mm(T[0][:, SEQ:SEQ + 1], attT[:, 3, :], bv[:, :]).then_inc(s_tr, 1)
            spread(0, 0, 1, 1)
            center_x(1, 2)
            pe.wait_ge(s_pre, NPRE + 2)

            def sums(r, q, k, prev):
                if k >= LAG and (not isinstance(r, int) or r < ROUNDS):
                    sum_states(r, q, k - LAG)
                elif k < LAG and prev:
                    sum_states(r - 1, 1 - q, k - LAG + STEPS)

            def body(r, q, ln, nxt, prev, tail):
                for k in range(STEPS):
                    if nxt and k == 7:
                        gate_in(r + 1)
                    if k < LAG or k % (STEPS // NB) != LAG:
                        sums(r, q, k, prev)
                        slot(r, q, k, ln, nxt, prev, tail)
                    else:
                        slot(r, q, k, ln, nxt, prev, tail)
                        sums(r, q, k, prev)
                    if k + 4 < STEPS:
                        spread(r, q, k // 2 + 2, k % 2)
                    elif nxt:
                        spread(r + 1, 1 - q, k // 2 + 2 - CHUNKS, k % 2)

            def unit(m):
                if m == 0:
                    pe.wait_ge(Fv.sem, Fv.at("b2", 0))
                    pe.wait_ge(s_w1, 16)
                    up(0, 0, 0, Hid_first)
                elif m % 2:
                    if m == 1:
                        pe.wait_ge(s_yd, ROUNDS * 4)
                    if m // 2 + 1 < EXPERTS:
                        up(0, 0, m // 2 + 1, Hid_first)
                    route_pe(1, 1, m // 2)
                else:
                    if m == 2:
                        pe.wait_ge(s_w2, 16)
                    down(0, 0, m // 2 - 1, Ts_first)

            def drain(n):
                if n < LAG:
                    sums(ROUNDS, 0, n, True)
                slot(**drain_slot(n))
                if n >= FIRST_UNIT:
                    unit(n - FIRST_UNIT)

            rounds(pe, body, drain)

            pe.wait_ge(s_hr, EXPERTS * HC)
            pe.wait_ge(s_ac, EXPERTS * NTT)
            pe.wait_ge(Tv.sem, Tv.all(ROUNDS - 1))
            up(1, 1, 0)

            def expert_body(r, q, nxt):
                for e in range(EXPERTS):
                    if e + 1 < EXPERTS:
                        up(r, q, e + 1)
                    if nxt:
                        route_pe(r + 1, 1 - q, e)
                        if e + 1 == EXPERTS:
                            up(r + 1, 1 - q, 0)
                    down(r, q, e)

            expert_rounds(pe, expert_body)

        @block.scalar
        def _(act):
            A = act.activation
            act.preload_act_table_set(EXP_LN)
            def square(producer, name, r, mk, bank, to):
                act.wait_ge(producer.sem, producer.at(name, r))
                A(to[:, :], bank, ACT.Square).then_inc(mk.sem, 1)

            def inverse_root(producer, name, r, mk, ln, bank, to):
                act.wait_ge(producer.sem, producer.at(name, r))
                A(to[:, :], bank, ACT.Ln, bias=epsc[:, 0:1]).then_inc(mk.sem, 1)
                act.wait_ge(mk.sem, mk.at(ln, r))
                A(to[:, :], to[:, :], ACT.Exp, scale=-0.5).then_inc(mk.sem, 1)

            def copy_x(r):
                act.wait_ge(Ap.sem, Ap.at("tr", r))
                if not isinstance(r, int) or r:
                    act.wait_ge(Ag.sem, Ag.at("xr", r - 1))
                A(xT[:, :], M[1][:, :], ACT.Copy).then_inc(Aa.sem, 1)

            def scan_input(r):
                act.wait_ge(Av.sem, Av.at("h0a", r))
                A(hpad[:, :, TAPS - 1:], xn2[:, :].rearrange("p (b s) -> p b s", b=NB), ACT.Identity, bias=lnb[:, 0:1]).then_inc(Aa.sem, 1)

            def silus(r, q):
                for d in range(DT):
                    act.wait_ge(Ap.sem, Ap.at(f"cv{d}", r))
                    A(xh[:, q, d, :], M[d][:, :], ACT.Silu, bias=convb[:, d:d + 1]).then_inc(Aa.sem, 1)
                for d in range(DT):
                    act.wait_ge(Ap.sem, Ap.at(f"rs{d}", r))
                    A(sres[:, q, d, :], M[d][:, :], ACT.Silu).then_inc(Aa.sem, 1)
                act.preload_act_table_set(EXP_LN)

            def split(r, q, n):
                if n == 0:
                    act.wait_ge(Ap.sem, Ap.at("wx", r))
                    A(dtr[:, :], M[0][0:DTR, :], ACT.Copy).then_inc(Aa.sem, 1)
                if n == 1:
                    act.wait_ge(Ap.sem, Ap.at("wbc", r))
                    A(S[:, q, :], M[1][0:96, :], ACT.Copy).then_inc(Aa.sem, 1)
                if n == 2:
                    act.wait_ge(Av.sem, Av.at("r1", r))
                    A(S[32:64, q, :], left[32:64, :], ACT.Copy)
                    A(S[64:96, q, :], left[64:96, :], ACT.Copy).then_inc(Aa.sem, 1)
                if n == 3:
                    act.wait_ge(Av.sem, Av.at("r2", r))
                    A(S[64:96, q, :], left[64:96, :], ACT.Copy).then_inc(Aa.sem, 1)

            def log_part(r, d):
                act.wait_ge(Ap.sem, Ap.at(f"dt{d}", r))
                if not isinstance(r, int) or r:
                    act.wait_ge(Ag.sem, Ag.at(f"dt{d}", r - 1))
                A(soft[:, d, :], M[d][:, :], ACT.Abs, bias=bdt[:, d:d + 1]).then_inc(Aa.sem, 1)
                act.wait_ge(Aa.sem, Aa.at(f"az{d}", r))
                A(soft[:, d, :], soft[:, d, :], ACT.Exp, scale=-1.0).then_inc(Aa.sem, 1)
                act.wait_ge(Aa.sem, Aa.at(f"ea{d}", r))
                A(soft[:, d, :], soft[:, d, :], ACT.Ln, bias=onec[:, 0:1]).then_inc(Aa.sem, 1)

            def copy_spread(r, j, of):
                for half in range(2):
                    i = j * PIECES + of * 2 + half
                    act.wait_ge(s_sp, r * CHUNKS * PIECES + i + 1)
                    if half == 0 and later(r, j, 2):
                        act.wait_ge((s_u, s_pd)[of], r * STEPS + 2 * j - 2)
                    A((Bs, Cs)[of][:, j % 2, 2 * half:2 * half + 2, :], Rp[:, i % SPREADS, :, :], ACT.Copy).then_inc(s_cp, 1)

            def decays(r, q, k):
                g = r * STEPS + k
                b, c, d = step_of(k)
                if later(r, k, RING):
                    act.wait_ge(s_sc, g - RING + 1)
                if k < DT:
                    act.wait_ge(Ag.sem, Ag.at(f"dt{d}", r))
                for i in range(NC):
                    m = A(dA[:, k % RING, i, 1:SEQ], dtm[:, q, d, b * SEQ + 1:(b + 1) * SEQ], ACT.Exp,
                          scale=Aneg[:, d, c * NC + i:c * NC + i + 1])
                m.then_inc(s_ex, 1)

            def copy_c(r):
                act.wait_ge(Tp.sem, Tp.at("ctr", r))
                src = T[1][:, 0:P].rearrange("p (b k) -> p b k", b=NB)
                A(cT[:, :, :], src, ACT.Copy).then_inc(Ta.sem, 1)
                for b in range(NB):
                    m = A(cT2[:, b, :, :], src[:, b, :].unsqueeze(1).to_broadcast([P, 2, KEYS]), ACT.Copy)
                m.then_inc(Ta.sem, 1)

            def copy_max(r):
                act.wait_ge(Tp.sem, Tp.at("m", r))
                A(nmT[:, :], Tb[0:96, 0:NB * SEQ], ACT.Copy).then_inc(Ta.sem, 1)

            def exps(r, b, g):
                act.wait_ge(Tp.sem, Tp.at(f"st{b}{g}", r))
                for h in range(2):
                    hp = TRIO[g][h][0]
                    m = A(E[:, b, hp:hp + 2, :], T[h][:, :].rearrange("p (i s) -> p i s", i=2), ACT.Exp)
                m.then_inc(Ta.sem, 1)

            def weight_sums(r):
                act.wait_ge(Tp.sem, Tp.at("o", r))
                A(rden[:, :], T[1][:, :], ACT.Ln).then_inc(Ta.sem, 1)
                act.wait_ge(Ta.sem, Ta.at("ld", r))
                A(rden[:, :], rden[:, :], ACT.Exp, scale=-1.0).then_inc(Ta.sem, 1)

            def route_act(r, q, e, G=G):
                if e == 0:
                    square(Fp, "cen", r, Fa, G[1], sq)
                if e == 1:
                    inverse_root(Fp, "var", r, Fa, "ln", G[0], rstd)
                if e == 3:
                    act.wait_ge(Fv.sem, Fv.at("sb", r))
                    A(pr[:, :, :], lg[:, :, :], ACT.Exp).then_inc(Fa.sem, 1)
                if e == 4:
                    act.wait_ge(Fv.sem, Fv.at("gap", r))
                    A(wt[:, 1, :], gap[:, :], ACT.Exp).then_inc(Fa.sem, 1)
                if e == 6:
                    act.wait_ge(Fp.sem, Fp.at("wT", r))
                    A(wselT[:, :], G[0][0:EXPERTS, :], ACT.Copy).then_inc(Fa.sem, 1)

            def relus(r, e, Hid=Hid):
                for j in range(HC):
                    i = e * HC + j
                    act.wait_ge(s_h, r * EXPERTS * HC + i + 1)
                    if j == 0 and (e >= 2 or not isinstance(r, int) or r):
                        act.wait_ge(s_o, r * EXPERTS + e - 1)
                    A(hid[e % 2][:, j, :], Hid[i % len(Hid)], ACT.Relu, bias=b1T[:, i:i + 1]).then_inc(s_hr, 1)

            def slot(r, q, k, ln, nxt, prev, tail):
                if tail:
                    if k < 2:
                        exps(r - 2, 1, k)
                    if k == 2:
                        weight_sums(r - 2)
                if prev:
                    if k == 5:
                        copy_c(r - 1)
                        square(Tp, "cen", r - 1, Ta, T[0][:, :], sqt)
                    if k == 7:
                        inverse_root(Tp, "var", r - 1, Ta, "ln", T[1][:, :], rstdt)
                    if k == 13:
                        copy_max(r - 1)
                    if k >= 14:
                        exps(r - 1, 0, k - 14)
                if nxt and k == 6:
                    silus(r + 1, 1 - q)
                if nxt:
                    if k == 0:
                        inverse_root(Ap, "var2", r + 1, Aa, "ln2", M[1][:, :], rstd)
                    if k == 1:
                        scan_input(r + 1)
                    if 7 <= k < 11:
                        split(r + 1, 1 - q, k - 7)
                    if 9 <= k < 11:
                        log_part(r + 1, k - 9)
                if ln:
                    if k == 12:
                        copy_x(r + 2)
                    if k == 13:
                        square(Ap, "cen1", r + 2, Aa, M[0][:, :], sq)
                    if k == 14:
                        inverse_root(Ap, "var1", r + 2, Aa, "ln1", M[1][:, :], rstd)
                    if k == 15:
                        square(Ap, "cen2", r + 2, Aa, M[0][:, :], sq)
                if is_last(r) and k % 2:
                    route_act(0, 0, k // 2, G_first)

            act.wait_ge(s_pre, 1)
            act.wait_ge(s_first, FIRST)
            copy_x(0)
            for n in (1, 2):
                square(Ap, f"cen{n}", 0, Aa, M[0][:, :], sq)
                inverse_root(Ap, f"var{n}", 0, Aa, f"ln{n}", M[1][:, :], rstd)
            scan_input(0)
            act.wait_ge(s_w, WALL)
            A(Aneg[:, :, :], alog[:, :, :], ACT.Exp).then_inc(s_prea, 1)

            def copy_weights(first, last):
                for i in range(first, last):
                    src, dst, rows, cols = turns[i]
                    act.wait_ge(s_tr, i + 1)
                    v = T[i % 2][0:cols, 0:src.shape[1] * rows].rearrange("p (n c) -> p n c", c=rows)
                    if isinstance(dst, int):
                        A(wdtrT[:, dst, :], v[:, 0, 0:DTR], ACT.Copy)
                        A(wbcT[:, dst, :, :], v[:, :, DTR:96].to_broadcast([P, 3, 2 * NST]), ACT.Copy).then_inc(s_tc, 1)
                    else:
                        A(dst, v, ACT.Copy).then_inc(s_tc, 1)

            copy_weights(0, MIXER)
            silus(0, 0)
            act.wait_ge(s_pre, NPRE)
            split(0, 0, 0)
            split(0, 0, 1)
            split(0, 0, 2)
            log_part(0, 0)
            split(0, 0, 3)
            log_part(0, 1)
            copy_spread(0, 0, 0)
            decays(0, 0, 0)
            copy_spread(0, 0, 1)
            decays(0, 0, 1)
            copy_spread(0, 1, 0)
            decays(0, 0, 2)
            copy_x(1)
            square(Ap, "cen1", 1, Aa, M[0][:, :], sq)
            copy_weights(MIXER, NTURN)
            inverse_root(Ap, "var1", 1, Aa, "ln1", M[1][:, :], rstd)
            square(Ap, "cen2", 1, Aa, M[0][:, :], sq)

            def body(r, q, ln, nxt, prev, tail):
                for k in range(STEPS):
                    more = k + 3 < STEPS
                    if more or nxt:
                        rr, qq, kk = (r, q, k + 3) if more else (r + 1, 1 - q, k + 3 - STEPS)
                        copy_spread(rr, kk // 2, kk % 2)
                        decays(rr, qq, kk)
                    slot(r, q, k, ln, nxt, prev, tail)

            def drain(n):
                slot(**drain_slot(n))
                m = n - FIRST_UNIT
                if m == 0:
                    relus(0, 0, Hid_first)
                elif m > 0 and m % 2:
                    if m // 2 + 1 < EXPERTS:
                        relus(0, m // 2 + 1, Hid_first)
                    route_act(1, 1, m // 2)

            rounds(act, body, drain)
            relus(1, 0)

            def expert_body(r, q, nxt):
                for e in range(EXPERTS):
                    if e + 1 < EXPERTS:
                        relus(r, e + 1)
                    if nxt:
                        route_act(r + 1, 1 - q, e)
                        if e + 1 == EXPERTS:
                            relus(r + 1, 0)

            expert_rounds(act, expert_body)

        @block.gpsimd
        def _(pool):
            TT = pool.tensor_tensor

            def residual(r, q):
                pool.wait_ge(Av.sem, Av.at("xn", r))
                if not isinstance(r, int) or r >= 2:
                    pool.wait_ge(s_x1, r - 1)
                TT(xres[:, q, :], xT[:, :], xn[:, :], ALU.add).then_inc(Ag.sem, 1)

            def steps_x(r, q, d):
                pool.wait_ge(Aa.sem, Aa.at(f"L{d}", r))
                pool.wait_ge(Av.sem, Av.at(f"zp{d}", r))
                TT(dtm[:, q, d, :], dtm[:, q, d, :], soft[:, d, :], ALU.add).then_inc(Ag.sem, 1)
                pool.wait_ge(Ag.sem, Ag.at(f"dt{d}", r))
                TT(dtx[:, q, d, :], dtm[:, q, d, :], xh[:, q, d, :], ALU.mult).then_inc(Ag.sem, 1)

            def inputs(r, q, k):
                b, c, d = step_of(k)
                if d == 0:
                    pool.wait_ge(s_cp, (r * CHUNKS + k // 2) * PIECES + 2)
                if k < DT:
                    pool.wait_ge(Ag.sem, Ag.at(f"dx{d}", r))
                if later(r, k, RING):
                    pool.wait_ge(s_sc, r * STEPS + k - RING + 1)
                TT(u[:, k % RING, :, :], Bs[:, (k // 2) % 2, :, :],
                   dtx[:, q, d, b * SEQ:(b + 1) * SEQ].unsqueeze(1).to_broadcast([P, NC, SEQ]), ALU.mult).then_inc(s_u, 1)

            def fold(r, k):
                pool.wait_ge(s_pd, r * STEPS + k + 1)
                TT(prod[:, k % RING, 0:NC // 2, :], prod[:, k % RING, 0:NC // 2, :], prod[:, k % RING, NC // 2:NC, :], ALU.add).then_inc(s_fd, 1)

            def gate(r, q, b):
                for d in range(DT):
                    pool.wait_ge(s_yd, r * 4 + 2 * b + d + 1)
                    if b == 0 and d == 0 and (not isinstance(r, int) or r):
                        pool.wait_ge(s_wo, r)
                    TT(gy[:, d, b * SEQ:(b + 1) * SEQ], yd[:, d, :], sres[:, q, d, b * SEQ:(b + 1) * SEQ], ALU.mult).then_inc(s_gy, 1)

            def key_blocks(r, b):
                pool.wait_ge(Tv.sem, Tv.at("KT", r))
                TT(Kbd[:, b, :, :], KT[:, b, :].unsqueeze(1).to_broadcast([P, HEADS, KEYS]),
                   blk[:, :].unsqueeze(2).to_broadcast([P, HEADS, KEYS]), ALU.mult).then_inc(Tg.sem, 1)

            def slot(r, q, k, ln, nxt, prev, tail):
                if k == 10 and (not isinstance(r, int) or r < ROUNDS):
                    gate(r, q, 0)
                if prev:
                    if k == 3:
                        gate(r - 1, 1 - q, 1)
                    if 7 <= k < 9:
                        key_blocks(r - 1, k - 7)
                if nxt:
                    if k == 5:
                        residual(r + 1, 1 - q)
                    if 10 <= k < 12:
                        steps_x(r + 1, 1 - q, k - 10)

            pool.wait_ge(s_w, WALL)
            residual(0, 0)
            for d in range(DT):
                steps_x(0, 0, d)
            inputs(0, 0, 0)
            inputs(0, 0, 1)

            def body(r, q, ln, nxt, prev, tail):
                for k in range(STEPS):
                    if k + 2 < STEPS:
                        inputs(r, q, k + 2)
                    elif nxt:
                        inputs(r + 1, 1 - q, k + 2 - STEPS)
                    if k:
                        fold(r, k - 1)
                    elif prev:
                        fold(r - 1, STEPS - 1)
                    slot(r, q, k, ln, nxt, prev, tail)

            def drain(n):
                if n == 0:
                    fold(ROUNDS - 1, STEPS - 1)
                slot(**drain_slot(n))

            rounds(pool, body, drain)

        @block.vector
        def _(v):
            v.memset(Vg[:, :, :, :], 0.0)
            v.memset(ones[:, :, :], 0.0).then_inc(s_pres, 1)
            v.wait_ge(s_pres, 1)
            for i in range(2):
                for h in range(2):
                    v.memset(ones[64 * h:64 * h + 64, i, (2 * i + h) * HD:(2 * i + h + 1) * HD], 1.0)
            v.memset(hpad[:, :, 0:TAPS - 1], 0.0)
            v.memset(dA[:, :, :, 0:1], 0.0)
            v.memset(nm[:, :, :, :], 0.0)
            v.memset(epsc[:, :], EPS)
            v.memset(onec[:, :], 1.0).then_inc(s_pre, 1)
            def normed(r, n):
                v.wait_ge(Aa.sem, Aa.at(f"rs{n}", r))
                if n == 1:
                    v.tensor_tensor(xn[:, :], M[0][:, :], rstd[:, :], ALU.mult).then_inc(Av.sem, 1)
                else:
                    v.scalar_tensor_tensor(xn2[:, :], M[0][:, :], lng[:, 0:1], rstd[:, :], ALU.mult, ALU.mult).then_inc(Av.sem, 1)

            def rest(r, q, n):
                if n == 1:
                    v.wait_ge(Aa.sem, Aa.at("S1", r))
                    v.tensor_tensor(left[:, :], M[1][0:96, :], S[:, q, :], ALU.subtract).then_inc(Av.sem, 1)
                else:
                    v.wait_ge(Aa.sem, Aa.at("S2", r))
                    v.tensor_tensor(left[64:96, :], left[64:96, :], S[64:96, q, :], ALU.subtract).then_inc(Av.sem, 1)

            def positive(r, q, d):
                v.wait_ge(Aa.sem, Aa.at(f"az{d}", r))
                v.tensor_scalar(dtm[:, q, d, :], M[d][:, :], bdt[:, d:d + 1], 0.0, ALU.add, ALU.max).then_inc(Av.sem, 1)

            def scan(r, k):
                g = r * STEPS + k
                v.wait_ge(s_ex, g + 1)
                v.wait_ge(s_u, g + 1)
                if later(r, k, 2):
                    v.wait_ge(s_pd, g - 1)
                v.tensor_tensor_scan(hst[:, k % 2].rearrange("p n s -> p (n s)"), dA[:, k % RING].rearrange("p n s -> p (n s)"),
                                     u[:, k % RING].rearrange("p n s -> p (n s)"), 0.0, ALU.mult, ALU.add).then_inc(s_sc, 1)

            def times_c(r, k):
                g = r * STEPS + k
                v.wait_ge(s_sc, g + 1)
                v.wait_ge(s_cp, (r * CHUNKS + k // 2 + 1) * PIECES)
                if later(r, k, RING):
                    v.wait_ge(s_ns, g - RING + 1)
                v.tensor_tensor(prod[:, k % RING, :, :], hst[:, k % 2, :, :], Cs[:, (k // 2) % 2, :, :], ALU.mult).then_inc(s_pd, 1)

            def skip(r, q, b):
                v.wait_ge(s_ns, r * STEPS + 8 * (b + 1))
                if b or not isinstance(r, int) or r:
                    v.wait_ge(s_gy, r * 4 + 2 * b)
                for d in range(DT):
                    v.scalar_tensor_tensor(yd[:, d, :], xh[:, q, d, b * SEQ:(b + 1) * SEQ], dpar[:, d:d + 1], Y[:, d, :],
                                           ALU.mult, ALU.add).then_inc(s_yd, 1)

            def mixer_out(r, q):
                v.wait_ge(s_wo, r + 1)
                if later(r):
                    v.wait_ge(Tv.sem, Tv.at("x2", r - 1))
                v.scalar_tensor_tensor(x1T[:, :], T[0][:, :], alph[:, 0:1], xres[:, q, :], ALU.mult, ALU.add).then_inc(s_x1, 1)

            def copy_kv(r):
                v.wait_ge(Tp.sem, Tp.at("kv", r))
                if later(r):
                    v.wait_ge(Tg.sem, Tg.at("kb1", r - 1))
                v.tensor_scalar(KT[:, :, :], T[1][:, 0:P].rearrange("p (b k) -> p b k", b=NB), bk[:, 0:1], None, ALU.add).then_inc(Tv.sem, 1)
                if later(r):
                    v.wait_ge(Tp.sem, Tp.at("o", r - 1))
                vals = T[1][:, P:P + NB * P].rearrange("p (b g i h e) -> p b g i h e", b=NB, i=2, h=2, e=HD)
                to = Vg[:, :, :, :].rearrange("p b (g i) w -> p b g i w", i=2)
                for i in range(2):
                    for h in range(2):
                        c, rows = (2 * i + h) * HD, slice(64 * h, 64 * h + 64)
                        m = v.tensor_copy(to[rows, :, :, i, c:c + HD], vals[rows, :, :, i, h, :])
                m.then_inc(Tv.sem, 1)

            def att_normed(r):
                v.wait_ge(Ta.sem, Ta.at("rs", r))
                v.tensor_tensor(xq[:, :], T[0][:, :], rstdt[:, :], ALU.mult).then_inc(Tv.sem, 1)

            def queries(r):
                v.wait_ge(Tp.sem, Tp.at("q", r))
                v.scalar_tensor_tensor(qT[:, :, :], T[1][:, :].rearrange("p (b s) -> p b s", b=NB), bq[:, 0:1],
                                       KA[:, :].unsqueeze(1).to_broadcast([P, NB, SEQ]), ALU.add, ALU.mult).then_inc(Tv.sem, 1)

            def maxima(r, i):
                for h in range(2):
                    v.wait_ge(Tp.sem, Tp.at(f"s{i}{'ab'[h]}", r))
                    v.tensor_reduce(mx[:, i, h * 8:h * 8 + 8], T[h][:, :].rearrange("p (h k) -> p h k", k=KEYS), AX.X, ALU.max).then_inc(Tv.sem, 1)

            def split_max(r):
                v.wait_ge(Tv.sem, Tv.at("mx3b", r))
                v.tensor_scalar(nm[:, :, 0, 0:HEADS], mx[:, :, :], -1.0, None, ALU.mult).then_inc(Tv.sem, 1)
                v.wait_ge(Tv.sem, Tv.at("ma", r))
                v.scalar_tensor_tensor(mleft[:, :, :], mx[:, :, :], -1.0, nm[:, :, 0, 0:HEADS], ALU.mult, ALU.subtract).then_inc(Tv.sem, 1)
                v.wait_ge(Tv.sem, Tv.at("mb", r))
                v.tensor_copy(nm[:, :, 1, 0:HEADS], mleft[:, :, :]).then_inc(Tv.sem, 1)
                v.wait_ge(Tv.sem, Tv.at("mc", r))
                v.tensor_tensor(mleft[:, :, :], mleft[:, :, :], nm[:, :, 1, 0:HEADS], ALU.subtract).then_inc(Tv.sem, 1)
                v.wait_ge(Tv.sem, Tv.at("md", r))
                v.tensor_copy(nm[:, :, 2, 0:HEADS], mleft[:, :, :]).then_inc(Tv.sem, 1)

            def normalise(r):
                v.wait_ge(Ta.sem, Ta.at("rd", r))
                v.tensor_tensor(oT[:, :], T[0][:, :], rden[:, :], ALU.mult).then_inc(Tv.sem, 1)

            def att_out(r):
                v.wait_ge(Tp.sem, Tp.at("wo", r))
                v.wait_ge(s_x2, 16 * (r + 1))
                v.scalar_tensor_tensor(x2o[:, :], T[1][:, :], bo[:, 0:1], x1T[:, :], ALU.add, ALU.add).then_inc(Tv.sem, 1)

            def route(r, q, e, G=G):
                def go(ins, name):
                    ins.then_inc(Fv.sem, 1)
                    v.wait_ge(Fv.sem, Fv.at(name, r))
                if e == 1:
                    v.wait_ge(Fa.sem, Fa.at("rs", r))
                    v.tensor_tensor(xf[q][:, :], G[1], rstd[:, :], ALU.mult).then_inc(Fv.sem, 1)
                if e == 2:
                    v.wait_ge(Fp.sem, Fp.at("g", r))
                    lp = G[0][:, 0:NTT * EXPERTS].rearrange("p (t e) -> p t e", t=NTT)
                    go(v.tensor_tensor(lg[:, :, :], lp, bgs[:, :].unsqueeze(1).to_broadcast([P, NTT, EXPERTS]), ALU.add), "lg")
                    go(v.tensor_reduce(lmax[:, :], lg[:, :, :], AX.X, ALU.max), "mx")
                    go(v.tensor_tensor(lg[:, :, :], lg[:, :, :], lmax[:, :].unsqueeze(2).to_broadcast([P, NTT, EXPERTS]), ALU.subtract), "sb")
                    v.wait_ge(Fp.sem, Fp.at("x2", r))
                    if not isinstance(r, int) or r >= 2:
                        v.wait_ge(s_out[q], 8 * (r - q))
                    go(v.tensor_copy(acc[q], G[1].rearrange("p (t d) -> p t d", t=NTT)), "x2")
                if e == 3:
                    v.wait_ge(Fa.sem, Fa.at("e", r))
                    go(v.tensor_reduce(lsum[:, :], pr[:, :, :], AX.X, ALU.add), "pe0")
                    go(v.reciprocal(lsum[:, :], lsum[:, :]), "rs")
                    go(v.tensor_tensor(pr[:, :, :], pr[:, :, :], lsum[:, :].unsqueeze(2).to_broadcast([P, NTT, EXPERTS]), ALU.mult), "pr")
                    v.memset(idle[:, 0:1], 0.0)
                    for t in range(NTT):
                        v.max(top[:, t, :], pr[:, t, :]).then_inc(Fv.sem, 1)
                    v.wait_ge(Fv.sem, Fv.at(f"t{NTT - 1}", r))
                    v.memset(idle[:, 1:2], 0.0)
                    for t in range(NTT):
                        v.max_index(topi[:, t, :], top[:, t, :], pr[:, t, :]).then_inc(Fv.sem, 1)
                    v.wait_ge(Fv.sem, Fv.at(f"i{NTT - 1}", r))
                    go(v.tensor_copy(topf[:, :, :], topi[:, :, 0:2]), "tf")
                    go(v.tensor_tensor(gap[:, :], top[:, :, 1], top[:, :, 0], ALU.subtract), "gap")
                if e == 5:
                    v.wait_ge(Fa.sem, Fa.at("ge", r))
                    go(v.tensor_scalar(wt[:, 0, :], wt[:, 1, :], 1.0, None, ALU.add), "gs")
                    go(v.reciprocal(wt[:, 0, :], wt[:, 0, :]), "w0")
                    go(v.tensor_tensor(wt[:, 1, :], wt[:, 1, :], wt[:, 0, :], ALU.mult), "w1")
                    ib = iota[:, :].unsqueeze(1).to_broadcast([P, NTT, EXPERTS])
                    for i in range(2):
                        go(v.tensor_tensor(hot[:, i, :, :], topf[:, :, i:i + 1].to_broadcast([P, NTT, EXPERTS]), ib, ALU.is_equal), f"h{i}")
                    for i in range(2):
                        go(v.tensor_tensor(hot[:, i, :, :], hot[:, i, :, :], wt[:, i, :].unsqueeze(2).to_broadcast([P, NTT, EXPERTS]), ALU.mult), f"g{i}")
                    go(v.tensor_tensor(wsel[:, q, :, :], hot[:, 0, :, :], hot[:, 1, :, :], ALU.add), "wsel")
                if e == 7:
                    v.wait_ge(Fp.sem, Fp.at("b2", r))
                    go(v.tensor_tensor(acc[q], acc[q], G[1].rearrange("p (t d) -> p t d", t=NTT), ALU.add), "b2")

            def add(r, q, e, Ts=Ts):
                v.wait_ge(s_o, r * EXPERTS + e + 1)
                if e:
                    v.wait_ge(s_ac, (r * EXPERTS + e) * NTT)
                for t in range(NTT):
                    v.scalar_tensor_tensor(acc[q][:, t, :], Ts[e % 2][:, t * P:(t + 1) * P], wsel[:, q, t, e:e + 1], acc[q][:, t, :],
                                           ALU.mult, ALU.add).then_inc(s_ac, 1)

            def slot(r, q, k, ln, nxt, prev, tail):
                if tail:
                    if k == 3:
                        normalise(r - 2)
                    if k == 4:
                        att_out(r - 2)
                if nxt and k == 9:
                    rest(r + 1, 1 - q, 1)
                if prev:
                    if k == 2:
                        skip(r - 1, 1 - q, 1)
                    if k == 4:
                        mixer_out(r - 1, 1 - q)
                    if k == 6:
                        copy_kv(r - 1)
                    if k == 8:
                        att_normed(r - 1)
                        queries(r - 1)
                    if 9 <= k < 13:
                        maxima(r - 1, k - 9)
                    if k == 12:
                        split_max(r - 1)
                if k == 9 and (not isinstance(r, int) or r < ROUNDS):
                    skip(r, q, 0)
                if nxt:
                    if k == 0 and isinstance(r, int) and r == 0:
                        normed(1, 1)
                        attention_scale()
                    if k == 1:
                        normed(r + 1, 2)
                    if k == 9:
                        positive(r + 1, 1 - q, 0)
                    if k == 10:
                        rest(r + 1, 1 - q, 2)
                        positive(r + 1, 1 - q, 1)
                if ln and k == 15:
                    normed(r + 2, 1)
                if is_last(r) and k % 2:
                    route(0, 0, k // 2, G_first)

            v.wait_ge(s_first, FIRST)
            normed(0, 1)
            v.wait_ge(s_w, WALL)
            for d in range(DT):
                for k in range(TAPS):
                    v.tensor_scalar(win_tap[:, d * TAPS + k, :], win_nat[:, d, :], convw[:, d, k:k + 1], None, ALU.mult).then_inc(s_pre, 1)
            normed(0, 2)
            n = 1 + DT * TAPS

            def nxt_(ins):
                nonlocal n
                n += 1
                ins.then_inc(s_pre, 1)
                v.wait_ge(s_pre, n)
            nxt_(v.tensor_copy(identb[:, :], ident[:, :]))
            nxt_(v.tensor_copy(sel[:, :, :], pick[:, :].unsqueeze(2).to_broadcast([96, 2 * NST, P])))
            nxt_(v.tensor_copy(selmax[:, :, :].rearrange("p g (h k) -> p (g h) k", h=2), pickmax[:, :].unsqueeze(2).to_broadcast([96, HEADS, KEYS])))
            v.wait_ge(s_prea, 1)
            nxt_(v.tensor_scalar(Aneg[:, :, :], Aneg[:, :, :], -1.0, None, ALU.mult))
            nxt_(v.tensor_scalar(keep[:, :, :], mask_i[:, :, :], 0.0, None, ALU.not_equal))
            nxt_(v.tensor_scalar(mbias[:, :, :], keep[:, :, :], -MASKED, MASKED, ALU.mult, ALU.add))
            for t in range(QT):
                nxt_(v.tensor_copy(mbias2[:, t, :, :], mbias[:, t, :].unsqueeze(1).to_broadcast([P, 2, KEYS])))
            nxt_(v.tensor_reduce(kany[:, :], keep[:, :, :], AX.X, ALU.max))
            nxt_(v.tensor_scalar(kany[:, :], kany[:, :], float(HD) ** -0.5, None, ALU.mult))
            nxt_(v.memset(kanyb[:, :, :], 1.0))
            for t in range(QT):
                nxt_(v.tensor_scalar(kanyb[:, t, :], kanyb[:, t, :], kany[:, t:t + 1], None, ALU.mult))
            assert n == NPRE
            rest(0, 0, 1)
            positive(0, 0, 0)
            rest(0, 0, 2)
            positive(0, 0, 1)
            scan(0, 0)

            def attention_scale():
                v.wait_ge(s_tr, NTURN + 1)
                nxt_(v.tensor_copy(KA[:, :], T[0][:, 0:SEQ]))
                nxt_(v.tensor_tensor(bo[:, :], bo[:, :], T[0][:, SEQ:SEQ + 1], ALU.add))

            def body(r, q, ln, nxt, prev, tail):
                for k in range(STEPS):
                    if k + 1 < STEPS:
                        scan(r, k + 1)
                    elif nxt:
                        scan(r + 1, 0)
                    times_c(r, k)
                    slot(r, q, k, ln, nxt, prev, tail)

            def drain(n):
                slot(**drain_slot(n))
                m = n - FIRST_UNIT
                if m > 0 and m % 2 == 0:
                    add(0, 0, m // 2 - 1, Ts_first)
                    route(1, 1, m // 2 - 1)

            rounds(v, body, drain)

            def expert_body(r, q, nxt):
                for e in range(EXPERTS):
                    add(r, q, e)
                    if nxt:
                        route(r + 1, 1 - q, e)

            expert_rounds(v, expert_body)


_INS = ['x', 'ctx_1024', 'mask_1x1xSxS2_ik0', 'L0_attn_ln_g', 'L0_attn_ln_b', 'L0_attn_W_in', 'L0_attn_W_x',
        'L0_attn_W_dt', 'L0_attn_b_dt', 'L0_attn_W_out', 'L0_attn_conv_w', 'L0_attn_conv_b', 'L0_attn_A_log',
        'L0_attn_D_param', 'L0_attn_alpha', 'L0_xattn_w_q', 'L0_xattn_b_q', 'L0_xattn_w_k', 'L0_xattn_b_k',
        'L0_xattn_w_v', 'L0_xattn_b_v', 'L0_xattn_w_o', 'L0_xattn_b_o', 'L0_ffn_W1', 'L0_ffn_b1', 'L0_ffn_W2',
        'L0_ffn_b2', 'L0_ffn_Wg', 'L0_ffn_bg']


def constants():
    import numpy as np
    eye = np.eye(P, dtype=np.float32)
    pick = np.tile(np.eye(2 * NST, dtype=np.float32), (3, 1))
    pickmax = np.tile(np.eye(32, HEADS, dtype=np.float32), (3, 1))
    blk = (np.arange(P)[:, None] // HD == np.arange(HEADS)[None]).astype(np.float32)
    iota = np.tile(np.arange(EXPERTS, dtype=np.float32), (P, 1))
    return {"ident": eye, "center": eye - np.float32(1.0 / D), "mean": np.full((P, P), 1.0 / D, np.float32),
            "pick": pick, "pickmax": pickmax, "blk": blk, "iota": iota}


def kernel(**inputs):
    import numpy as _np
    import concourse.bacc as _bacc
    from concourse import mybir as _mybir
    from concourse.bass_utils import run_bass_kernel_spmd as _run

    nc = _bacc.Bacc("TRN2", target_bir_lowering=False, num_devices=1)
    arrays, args = {}, []
    for name, a in [(n, inputs[n]) for n in _INS] + list(constants().items()):
        a = _np.ascontiguousarray(a)
        arrays[f"in_{name}"] = a
        args.append(nc.dram_tensor(f"in_{name}", a.shape, _mybir.dt.from_np(a.dtype), kind="ExternalInput").ap())
    args.append(nc.dram_tensor("out_0", (BATCH, SEQ, D), _mybir.dt.float32, kind="ExternalOutput").ap())
    decoder(nc, *args)
    r = _run(nc, [arrays], core_ids=[0])
    return r.results[0]["out_0"]
```
